# Optimizing a Trainium2 kernel written in Bass

```python
import numpy as np
import jax
import jax.numpy as jnp

def _softmax(x, axis=-1):
    return jax.nn.softmax(x, axis=axis)

def _gelu(x):
    return jax.nn.gelu(x, approximate=True)

def _silu(x):
    return jax.nn.silu(x)

def _sigmoid(x):
    return jax.nn.sigmoid(x)

def _layernorm(x, axis=-1, eps=1e-05):
    m = jnp.mean(x, axis=axis, keepdims=True)
    v = jnp.var(x, axis=axis, keepdims=True)
    return (x - m) / jnp.sqrt(v + eps)

def _scatter_add(tgt, idx, src, axis=0):
    return tgt.at[idx].add(src)

def _segment_sum(src, seg, n):
    return jax.ops.segment_sum(src, seg, n)
kernel_name = 'mk_decoder_postln_d1_seqx_r4_df812e'

def setup_inputs(seed: int=0):
    np.random.seed(seed)
    _w = jnp.asarray

    def _rec_inputs():
        import jax
        import jax.numpy as jnp
        _rk = jax.random.key(seed)
        x = 7.22e-05 + 1 * jax.random.normal(jax.random.fold_in(_rk, 1), (16, 256, 256), jnp.float32)
        _lenS = 256 - jax.random.randint(jax.random.fold_in(_rk, 7), (16,), 0, max(1, 256 // 4) + 1, jnp.int32)
        _lenS2 = 256 - jax.random.randint(jax.random.fold_in(_rk, 8), (16,), 0, max(1, 256 // 4) + 1, jnp.int32)
        _ctx_1024P = jax.random.normal(jax.random.fold_in(_rk, 11), (16, 16, 256), jnp.float32)
        _ctx_1024c = jax.random.dirichlet(jax.random.fold_in(_rk, 511), 0.3 * jnp.ones((16,), jnp.float32), (16, 256))
        _ctx_1024t = jnp.einsum('bsk,bkd->bsd', _ctx_1024c, _ctx_1024P)
        _ctx_1024t = _ctx_1024t * jax.lax.rsqrt(jnp.mean(jnp.square(_ctx_1024t)) + 1e-12) * 0.953939
        ctx_1024 = 4.13588e-05 + 0.999923 * (_ctx_1024t + 0.3 * jax.random.normal(jax.random.fold_in(_rk, 611), (16, 256, 256), jnp.float32))
        return (x, ctx_1024)
    x, ctx_1024 = _rec_inputs()

    def _L0_attn_setup():
        import jax, jax.numpy as jnp
        import numpy as np
        HEADS = 16
        DIM_HEAD = 64
        WINDOW = 128
        LOOK_BACKWARD = 1
        LOOK_FORWARD = 0
        THETA = 10000.0
        PAD_VALUE = -1

        def look_around(x, backward, forward, pad_value, axis):
            w = x.shape[axis]
            size = backward + forward + 1
            pads = [(0, 0)] * x.ndim
            pads[axis] = (backward, forward)
            p = jnp.pad(x, pads, constant_values=pad_value)
            segs = [jax.lax.slice_in_dim(p, s, s + w, axis=axis) for s in range(size)]
            return jnp.concatenate(segs, axis=axis + 1)

        def rotate_half(t):
            t1, t2 = jnp.split(t, 2, axis=-1)
            return jnp.concatenate([-t2, t1], axis=-1)
        key = jax.random.key(seed)
        k1, k2, k3 = jax.random.split(key, 3)
        dim = 256
        x = jax.random.normal(k1, (4, 1024, dim), dtype=jnp.float32)
        W_qkv = jax.random.normal(k2, (dim, 3 * HEADS * DIM_HEAD), dtype=jnp.float32) * dim ** (-0.5)
        W_out = jax.random.normal(k3, (HEADS * DIM_HEAD, dim), dtype=jnp.float32) * (HEADS * DIM_HEAD) ** (-0.5)
        return {'x': x, 'W_qkv': W_qkv, 'W_out': W_out}
    _L0_attn_all = _L0_attn_setup()
    _L0_attn_in = {k: v for k, v in _L0_attn_all.items() if k in ('W_qkv', 'W_out')}
    del _L0_attn_all

    def _L0_xattn_setup():
        import jax, jax.numpy as jnp
        import numpy as np
        B, S, E, A = (4, 512, 256, 256)
        key = jax.random.key(seed)
        ks = jax.random.split(key, 6)
        scale = 1.0 / np.sqrt(E)
        return {'query': jax.random.normal(ks[0], (B, S, E), jnp.float32), 'key': jax.random.normal(ks[1], (B, S, E), jnp.float32), 'value': jax.random.normal(ks[2], (B, S, E), jnp.float32), 'Wq': jax.random.normal(ks[3], (E, A), jnp.float32) * scale, 'bq': jnp.zeros((A,), jnp.float32), 'Wk': jax.random.normal(ks[4], (E, A), jnp.float32) * scale, 'bk': jnp.zeros((A,), jnp.float32), 'Wv': jax.random.normal(ks[5], (E, A), jnp.float32) * scale, 'bv': jnp.zeros((A,), jnp.float32)}
    _L0_xattn_all = _L0_xattn_setup()
    _L0_xattn_in = {k: v for k, v in _L0_xattn_all.items() if k in ('Wq', 'bq', 'Wk', 'bk', 'Wv', 'bv')}
    del _L0_xattn_all

    def _L0_ffn_setup():
        import jax, jax.numpy as jnp
        import numpy as np
        import math
        DIM = 256
        NUM_HEADS = 16
        SHARED_HEADS = 1
        ROUTED_HEADS = 3
        HEAD_DIM = DIM // NUM_HEADS
        B, N = (2, 512)
        key = jax.random.key(seed)
        ks = jax.random.split(key, 16)
        s = 1.0 / math.sqrt(DIM)
        inp = {'x': jax.random.normal(ks[0], (B, N, DIM), dtype=jnp.float32), 'Wq': jax.random.uniform(ks[1], (DIM, DIM), minval=-s, maxval=s), 'bq': jax.random.uniform(ks[2], (DIM,), minval=-s, maxval=s), 'Wk': jax.random.uniform(ks[3], (DIM, DIM), minval=-s, maxval=s), 'bk': jax.random.uniform(ks[4], (DIM,), minval=-s, maxval=s), 'Wv': jax.random.uniform(ks[5], (DIM, DIM), minval=-s, maxval=s), 'bv': jax.random.uniform(ks[6], (DIM,), minval=-s, maxval=s), 'Wp': jax.random.uniform(ks[7], (DIM, DIM), minval=-s, maxval=s), 'bp': jax.random.uniform(ks[8], (DIM,), minval=-s, maxval=s), 'Wr': jax.random.uniform(ks[9], (NUM_HEADS - SHARED_HEADS, DIM), minval=-s, maxval=s), 'br': jax.random.uniform(ks[10], (NUM_HEADS - SHARED_HEADS,), minval=-s, maxval=s), 'Ws': jax.random.uniform(ks[11], (2, DIM), minval=-s, maxval=s), 'bs': jax.random.uniform(ks[12], (2,), minval=-s, maxval=s), 'temperature': jnp.full((NUM_HEADS, 1, 1), float(np.log(np.expm1(1.0 / 0.24))), dtype=jnp.float32), 'query_embedding': 0.02 * jax.random.normal(ks[13], (NUM_HEADS, 1, HEAD_DIM), dtype=jnp.float32)}
        return inp
    _L0_ffn_all = _L0_ffn_setup()
    _L0_ffn_in = {k: v for k, v in _L0_ffn_all.items() if k in ('Wq', 'bq', 'Wk', 'bk', 'Wv', 'bv', 'Wp', 'bp', 'Wr', 'br', 'Ws', 'bs', 'temperature', 'query_embedding')}
    del _L0_ffn_all
    return {'x': x, 'ctx_1024': ctx_1024, 'L0_attn_W_qkv': _L0_attn_in['W_qkv'], 'L0_attn_W_out': _L0_attn_in['W_out'], 'L0_xattn_Wq': _L0_xattn_in['Wq'], 'L0_xattn_bq': _L0_xattn_in['bq'], 'L0_xattn_Wk': _L0_xattn_in['Wk'], 'L0_xattn_bk': _L0_xattn_in['bk'], 'L0_xattn_Wv': _L0_xattn_in['Wv'], 'L0_xattn_bv': _L0_xattn_in['bv'], 'L0_ffn_Wq': _L0_ffn_in['Wq'], 'L0_ffn_bq': _L0_ffn_in['bq'], 'L0_ffn_Wk': _L0_ffn_in['Wk'], 'L0_ffn_bk': _L0_ffn_in['bk'], 'L0_ffn_Wv': _L0_ffn_in['Wv'], 'L0_ffn_bv': _L0_ffn_in['bv'], 'L0_ffn_Wp': _L0_ffn_in['Wp'], 'L0_ffn_bp': _L0_ffn_in['bp'], 'L0_ffn_Wr': _L0_ffn_in['Wr'], 'L0_ffn_br': _L0_ffn_in['br'], 'L0_ffn_Ws': _L0_ffn_in['Ws'], 'L0_ffn_bs': _L0_ffn_in['bs'], 'L0_ffn_temperature': _L0_ffn_in['temperature'], 'L0_ffn_query_embedding': _L0_ffn_in['query_embedding']}

def reference(x, ctx_1024, L0_attn_W_qkv, L0_attn_W_out, L0_xattn_Wq, L0_xattn_bq, L0_xattn_Wk, L0_xattn_bk, L0_xattn_Wv, L0_xattn_bv, L0_ffn_Wq, L0_ffn_bq, L0_ffn_Wk, L0_ffn_bk, L0_ffn_Wv, L0_ffn_bv, L0_ffn_Wp, L0_ffn_bp, L0_ffn_Wr, L0_ffn_br, L0_ffn_Ws, L0_ffn_bs, L0_ffn_temperature, L0_ffn_query_embedding):
    import jax
    import jax.numpy as jnp

    def _L0_attn_ref(x, W_qkv, W_out):
        import jax, jax.numpy as jnp
        import numpy as np
        HEADS = 16
        DIM_HEAD = 64
        WINDOW = 128
        LOOK_BACKWARD = 1
        LOOK_FORWARD = 0
        THETA = 10000.0
        PAD_VALUE = -1

        def look_around(x, backward, forward, pad_value, axis):
            w = x.shape[axis]
            size = backward + forward + 1
            pads = [(0, 0)] * x.ndim
            pads[axis] = (backward, forward)
            p = jnp.pad(x, pads, constant_values=pad_value)
            segs = [jax.lax.slice_in_dim(p, s, s + w, axis=axis) for s in range(size)]
            return jnp.concatenate(segs, axis=axis + 1)

        def rotate_half(t):
            t1, t2 = jnp.split(t, 2, axis=-1)
            return jnp.concatenate([-t2, t1], axis=-1)
        b, n, dim = x.shape
        h, dh, ws = (HEADS, DIM_HEAD, WINDOW)
        w = n // ws
        j = ws * (LOOK_BACKWARD + LOOK_FORWARD + 1)
        qkv = x @ W_qkv
        q, k, v = jnp.split(qkv, 3, axis=-1)

        def to_bhwnd(t):
            return t.reshape(b, n, h, dh).transpose(0, 2, 1, 3).reshape(b, h, w, ws, dh)
        bq = to_bhwnd(q) * dh ** (-0.5)
        bk = look_around(to_bhwnd(k), LOOK_BACKWARD, LOOK_FORWARD, float(PAD_VALUE), axis=2)
        bv = look_around(to_bhwnd(v), LOOK_BACKWARD, LOOK_FORWARD, float(PAD_VALUE), axis=2)
        inv_freq = 1.0 / THETA ** (jnp.arange(0, dh, 2, dtype=jnp.float32) / dh)
        t_pos = jnp.arange(j, dtype=jnp.float32)
        freqs = t_pos[:, None] * inv_freq[None, :]
        freqs = jnp.concatenate([freqs, freqs], axis=-1)
        q_freqs = freqs[-ws:]
        bq = bq * jnp.cos(q_freqs) + rotate_half(bq) * jnp.sin(q_freqs)
        bk = bk * jnp.cos(freqs) + rotate_half(bk) * jnp.sin(freqs)
        sim = jnp.einsum('bhwid,bhwjd->bhwij', bq, bk)
        seq = jnp.arange(n).reshape(w, ws)
        bq_t = seq[:, :, None]
        bq_k = look_around(seq[None], LOOK_BACKWARD, LOOK_FORWARD, PAD_VALUE, axis=1)[0]
        bq_k = bq_k[:, None, :]
        pad_mask = bq_k == PAD_VALUE
        causal_mask = (bq_t < bq_k) | (bq_t > bq_k + ws * LOOK_BACKWARD)
        mask = causal_mask | pad_mask
        mask_value = -jnp.finfo(sim.dtype).max
        sim = jnp.where(mask, mask_value, sim)
        attn = jax.nn.softmax(sim, axis=-1)
        out = jnp.einsum('bhwij,bhwjd->bhwid', attn, bv)
        out = out.reshape(b, h, n, dh).transpose(0, 2, 1, 3).reshape(b, n, h * dh)
        return out @ W_out

    def _L0_xattn_ref(query, key, value, Wq, bq, Wk, bk, Wv, bv):
        import jax, jax.numpy as jnp
        import numpy as np
        B, S, E, A = (4, 512, 256, 256)
        q = jnp.einsum('bse,ea->bsa', query, Wq) + bq
        k = jnp.einsum('bse,ea->bsa', key, Wk) + bk
        v = jnp.einsum('bse,ea->bsa', value, Wv) + bv
        inv_sqrt_d = 1.0 / jnp.sqrt(jnp.asarray(A, q.dtype))
        scores = jnp.einsum('bqa,bka->bqk', q, k) * inv_sqrt_d
        probs = jax.nn.softmax(scores, axis=-1)
        return jnp.einsum('bqk,bka->bqa', probs, v)

    def _L0_ffn_ref(x, Wq, bq, Wk, bk, Wv, bv, Wp, bp, Wr, br, Ws, bs, temperature, query_embedding):
        import jax, jax.numpy as jnp
        import numpy as np
        import math
        DIM = 256
        NUM_HEADS = 16
        SHARED_HEADS = 1
        ROUTED_HEADS = 3
        HEAD_DIM = DIM // NUM_HEADS
        B, N = (2, 512)
        Bsz, Nn, C = x.shape
        H, hd = (NUM_HEADS, HEAD_DIM)

        def heads(W, b):
            y = x @ W.T + b
            return y.reshape(Bsz, Nn, H, hd).transpose(0, 2, 1, 3)
        q = heads(Wq, bq)
        k = heads(Wk, bk)
        v = heads(Wv, bv)
        q_norm = q / jnp.linalg.norm(q, axis=-1, keepdims=True)
        q_scaled = (q_norm + query_embedding[None]) * jax.nn.softplus(temperature)[None]
        attn = jnp.einsum('bhqd,bhkd->bhqk', q_scaled, k) / math.sqrt(hd)
        attn = jax.nn.softmax(attn, axis=-1)
        h = jnp.einsum('bhqk,bhkd->bhqd', attn, v)
        h = h.transpose(0, 2, 1, 3).reshape(Bsz, Nn, C)
        gates = jax.nn.softmax(h @ Wr.T + br, axis=-1)
        _, idx = jax.lax.top_k(gates, ROUTED_HEADS)
        mask = jax.nn.one_hot(idx, H - SHARED_HEADS, dtype=gates.dtype).sum(axis=-2)
        routed_gates = gates * mask * ROUTED_HEADS
        sw = jax.nn.softmax(h @ Ws.T + bs, axis=-1)
        shared_gates = sw * SHARED_HEADS
        weight_0 = sw * 2.0
        shared_gates = weight_0[..., 0:1] * shared_gates
        routed_gates = weight_0[..., 1:2] * routed_gates
        masked_gates = jnp.concatenate([shared_gates, routed_gates], axis=-1)
        out = h * masked_gates.sum(axis=-1, keepdims=True)
        return out @ Wp.T + bp
    x = _layernorm(x + _L0_attn_ref(x, L0_attn_W_qkv, L0_attn_W_out), axis=-1)
    x = _layernorm(x + _L0_xattn_ref(x, ctx_1024, ctx_1024, L0_xattn_Wq, L0_xattn_bq, L0_xattn_Wk, L0_xattn_bk, L0_xattn_Wv, L0_xattn_bv), axis=-1)
    x = _layernorm(x + _L0_ffn_ref(x, L0_ffn_Wq, L0_ffn_bq, L0_ffn_Wk, L0_ffn_bk, L0_ffn_Wv, L0_ffn_bv, L0_ffn_Wp, L0_ffn_bp, L0_ffn_Wr, L0_ffn_br, L0_ffn_Ws, L0_ffn_bs, L0_ffn_temperature, L0_ffn_query_embedding), axis=-1)
    return x

_drawn_inputs = setup_inputs


def setup_inputs(seed=0):
    import zlib

    import numpy as np

    out = dict(_drawn_inputs(seed))
    spreads = {'L0_xattn_bq': (0.0, 0.349),
     'L0_xattn_bk': (0.0, 2.0),
     'L0_xattn_bv': (0.0, 0.1),
     'L0_ffn_temperature': (4.151041507720947, 0.6)}
    factors = {'L0_ffn_bq': 8.0,
     'L0_ffn_bk': 64.0,
     'L0_ffn_Wr': 6.164,
     'L0_ffn_br': 8.0,
     'L0_ffn_Ws': 8.0,
     'L0_ffn_bs': 40.909,
     'L0_ffn_query_embedding': 8.0}
    for name, (base, spread) in spreads.items():
        noise = np.random.default_rng([zlib.crc32(name.encode()), seed]).standard_normal(out[name].shape)
        drawn = base * np.exp(spread * noise) if base else spread * noise
        out[name] = jnp.asarray(drawn.astype(out[name].dtype))
    for name, factor in factors.items():
        out[name] = (out[name] * factor).astype(out[name].dtype)
    return out
```

```python
from contextlib import ExitStack

import concourse.bass as bass
from concourse import mybir

F32 = mybir.dt.float32
ALU = mybir.AluOpType
ACT = mybir.ActivationFunctionType
AX = mybir.AxisListType

P = 128
B = 16
N = 256
C = 256
T = N // P
KC = C // P
H1, D1 = 16, 64
E1 = H1 * D1
PAIRS = H1 // 2
H3, D3 = 16, 16
HT = P // D3
NR, NS = 15, 2
NG = NR + NS
TOPK = 3
BANK = 512
EPS = 1e-5
CHUNKS = E1 // BANK
BIG = 3.0e38

HEADS = [("self", h) for h in range(H1)] + [("cross", 0)] + [("moh", h) for h in range(H3)]
INDEX = {head: n for n, head in enumerate(HEADS)}
P_SLOTS, PT_SLOTS, S_SLOTS = 3, 2, 3
LAG_T, LAG_PV = 2, 3


class Ring:

    def __init__(self, banks, ready, order, read_out):
        self.banks, self.ready, self.order, self.read_out = banks, ready, order, read_out

    def bank(self, item):
        return self.banks[self.order.index(item) % len(self.banks)]

    def is_ready(self, item):
        n, r = self.order.index(item), len(self.banks)
        return self.ready[n % r], n // r + 1

    def filled(self, item):
        return self.ready[self.order.index(item) % len(self.banks)]

    def take(self, pe, item):
        n, r = self.order.index(item), len(self.banks)
        if n >= r:
            pe.wait_ge(*self.read_out[self.order[n - r]])
        return self.banks[n % r]


def decoder_layer(nc, x, ctx_in, w_qkv, w_out, xwq, xbq, xwk, xbk, xwv, xbv, fwq, fbq, fwk, fbk,
                  fwv, fbv, fwp, fbp, gate_w, gate_b, temperature, query_embedding,
                  rope, mask, identity, out):
    with ExitStack() as ctx:
        def sb(name, *shape):
            return ctx.enter_context(nc.sbuf_tensor(name, list(shape), F32))

        def sem(name):
            return ctx.enter_context(nc.semaphore(name))

        wqkv_s = sb("wqkv_s", P, KC, 3 * E1)
        wout_s = sb("wout_s", P, PAIRS, C)
        square = {n: sb(n + "_s", P, KC, C) for n in ("xwq", "xwk", "xwv", "fwq", "fwk", "fwv", "fwp")}
        gate_ws = sb("gate_ws", P, KC, NG)
        gate_bs = sb("gate_bs", P, NG)
        column = {n: sb(n + "_c", P, KC) for n in ("xbq", "xbk", "fbk")}
        row = {n: sb(n + "_r", P, C) for n in ("xbv", "fbq", "fbv", "fbp", "qe")}
        temp_s = sb("temp_s", P, H3)
        soft = sb("soft", P, 6, H3)
        head_scale = sb("head_scale", P, H3)
        rope_s = sb("rope_s", P, T, 2, 2, D1)
        mask_s = sb("mask_s", P, 3 * P)
        ident = sb("ident", P, P)
        power = sb("power", P, T * H3)

        x_in = sb("x_in", P, T, C)
        c_in = sb("c_in", P, T, C)
        x_t = sb("x_t", P, KC, N)
        c_t = sb("c_t", P, KC, N)
        rope_cos = sb("rope_cos", P, 2, BANK)
        rope_sin = sb("rope_sin", P, 2, BANK)
        qk_rot = sb("qk_rot", P, T, 2 * E1)
        v1 = sb("v1", P, T, E1)
        q_pad = sb("q_pad", P, 2, 2, N)
        k_t = sb("k_t", P, 2, N)
        scores = sb("scores", P, S_SLOTS, 3 * P)
        neg_max = sb("neg_max", P, len(HEADS), T)
        row_sum = sb("row_sum", P, len(HEADS), T)
        row_inv = sb("row_inv", P, len(HEADS), T)
        probs = sb("probs", P, P_SLOTS, T * N)
        probs_t = sb("probs_t", P, PT_SLOTS, T * N)
        o_t = sb("o_t", P, PAIRS, N)
        z = sb("z", P, 3, T, C)
        stats = sb("stats", P, 3, T, 6)
        moments = sb("moments", P, 3, T, 2)
        var_eps = sb("var_eps", P, 3, T)
        rstd = sb("rstd", P, 3, T)
        x1 = sb("x1", P, T, C)
        x1_t = sb("x1_t", P, KC, N)
        xq_t = sb("xq_t", P, KC, N)
        xk_t = sb("xk_t", P, KC, N)
        xv = sb("xv", P, T, C)
        x2 = sb("x2", P, T, C)
        x2_t = sb("x2_t", P, KC, N)
        fq = sb("fq", P, T, C)
        fq_sq = sb("fq_sq", P, T, C)
        fq_n = sb("fq_n", P, T, C)
        fq_e = sb("fq_e", P, T, C)
        fq_f = sb("fq_f", P, T, C)
        q_ss = sb("q_ss", P, T * H3)
        q_inv = sb("q_inv", P, T * H3)
        fq_t = sb("fq_t", P, KC, N)
        fk_t = sb("fk_t", P, KC, N)
        fq_pad = sb("fq_pad", P, H3, N)
        v_pad = sb("v_pad", P, T, H3, P)
        h_t = sb("h_t", P, KC, N)
        gates = sb("gates", P, 5, T, NG)
        gsmall = sb("gsmall", P, 12, T)
        top8 = sb("top8", P, T, 8)
        ffn = sb("ffn", P, T, C)
        out_s = sb("out_s", P, T, C)

        def ring(name, order, read_out, counted=True):
            banks = [ctx.enter_context(nc.psum_tensor(f"{name}{i}", [P, BANK], F32)) for i in range(2)]
            ready = [sem(f"{name}_ready{i}") for i in range(2)] if counted else []
            return Ring(banks, ready, order, read_out)

        w_loaded, x_loaded, c_loaded, out_stored = sem("w_loaded"), sem("x_loaded"), sem("c_loaded"), sem("out_stored")
        setup_dve, setup_act = sem("setup_dve"), sem("setup_act")

        dve_step = sem("dve_step")
        pool_step = sem("pool_step")
        x_t_done, c_t_done = sem("x_t_done"), sem("c_t_done")
        halves_done, rot_done = sem("halves_done"), sem("rot_done")
        v1_done, pair_done = sem("v1_done"), sem("pair_done")
        max_done, exp_done, inv_done, norm_done = sem("max_done"), sem("exp_done"), sem("inv_done"), sem("norm_done")
        probs_t_done, head_done = sem("probs_t_done"), sem("head_done")
        o_t_done = sem("o_t_done")
        moments_done, rstd_done, layer_done = sem("moments_done"), sem("rstd_done"), sem("layer_done")
        x1_t_done, x2_t_done = sem("x1_t_done"), sem("x2_t_done")
        xk_done, xv_done, xq_done = sem("xk_done"), sem("xv_done"), sem("xq_done")
        ss_done, q_inv_done, fq_done, fq_t_done, fq_pad_done = (
            sem("ss_done"), sem("q_inv_done"), sem("fq_done"), sem("fq_t_done"), sem("fq_pad_done"))
        fk_done, v_pad_done, h_t_done = sem("fk_done"), sem("v_pad_done"), sem("h_t_done")
        logits_done, gate_exp_done = sem("logits_done"), sem("gate_exp_done")
        x_used = sem("x_used")
        fq_sum_done, gate_sum_done, x1_used = sem("fq_sum_done"), sem("gate_sum_done"), sem("x1_used")

        lin_order = ["xT", "cT"]
        for t in range(T):
            lin_order += [("qk", t, j) for j in range(2 * CHUNKS)] + [("v", t, j) for j in range(CHUNKS)]
        lin_order += ["xk", "xv"] + [("qkT", p) for p in range(PAIRS)]
        lin_order += ["y", "x1T", "xq", "x2T", "fq", "fk", "fv", "fqT", "gate", "ffn"]
        read_out = {"xT": (x_t_done, 1), "cT": (c_t_done, 1), "xk": (xk_done, 1), "xv": (xv_done, 1),
                    "y": (x_used, 1), "x1T": (x1_t_done, 1), "xq": (xq_done, 1), "x2T": (x2_t_done, 1),
                    "fq": (fq_sum_done, 1), "fk": (fk_done, 1), "fv": (v_pad_done, 1), "fqT": (fq_t_done, 1),
                    "gate": (gate_sum_done, 1)}
        for t in range(T):
            read_out |= {("qk", t, j): (halves_done, t * 2 * CHUNKS + j + 1) for j in range(2 * CHUNKS)}
            read_out |= {("v", t, j): (v1_done, t * CHUNKS + j + 1) for j in range(CHUNKS)}
        read_out |= {("qkT", p): (pair_done, p + 1) for p in range(PAIRS)}
        lin = ring("lin", lin_order, read_out)
        sc = ring("sc", HEADS, {head: (max_done if head[0] == "self" else exp_done, n + 1) for n, head in enumerate(HEADS)})
        pt = ring("pt", HEADS, {head: (probs_t_done, n + 1) for n, head in enumerate(HEADS)})
        values_read = {("self", p): (o_t_done, p + 1) for p in range(PAIRS)} | {("cross", 0): (x1_used, 1)}
        values_read |= {("moh", t): (h_t_done, t + 1) for t in range(KC)}
        pv = ring("pv", list(values_read), values_read, counted=False)

        n_loads = 0
        with nc.Block() as block:
            @block.sync
            def _(sp):
                nonlocal n_loads
                loads = [(wqkv_s[:, :, :], w_qkv.rearrange("(k p) n -> p k n", p=P)),
                         (wout_s[:, :, :], w_out.rearrange("(k p) n -> p k n", p=P)),
                         (gate_ws[:, :, :], gate_w.rearrange("(k p) n -> p k n", p=P)),
                         (rope_s[:, :, :, :, :], rope), (mask_s[:, :], mask), (ident[:, :], identity)]
                for tile, w in zip(square.values(), (xwq, xwk, xwv, fwq, fwk, fwv, fwp)):
                    loads.append((tile[:, :, :], w.rearrange("(k p) n -> p k n", p=P)))
                for tile, v in zip(row.values(), (xbv, fbq, fbv, fbp, query_embedding)):
                    loads.append((tile[:, :], v.partition_broadcast(P)))
                loads.append((gate_bs[:, :], gate_b.partition_broadcast(P)))
                loads.append((temp_s[:, :], temperature.partition_broadcast(P)))
                for tile, v in zip(column.values(), (xbq, xbk, fbk)):
                    loads.append((tile[:, :], v))
                for dst, src in loads:
                    sp.dma_start(dst, src).then_inc(w_loaded, 16)
                n_loads = len(loads)
                sp.sem_inc(out_stored, 16)
                sp.dma_start(x_in[:, :, :], x[0].rearrange("(t p) c -> p t c", p=P)).then_inc(x_loaded, 16)
                sp.dma_start(c_in[:, :, :], ctx_in[0].rearrange("(t p) c -> p t c", p=P)).then_inc(c_loaded, 16)
                sp.wait_ge(w_loaded, 16 * n_loads)

            @block.vector
            def _(dve):
                for tile in (q_pad[:, :, :, :], fq_pad[:, :, :], v_pad[:, :, :, :]):
                    nc.vector.memset(tile, 0.0)
                nc.vector.memset(power[:, :], -0.5)
                count = [0]

                def step(ins):
                    count[0] += 1
                    ins.then_inc(setup_dve, 1)
                    dve.wait_ge(setup_dve, count[0])

                u, w, ln_w, d, e, tmp = (soft[:, i, :] for i in range(6))
                dve.wait_ge(w_loaded, 16 * n_loads)
                step(nc.vector.tensor_scalar(tmp, temp_s[:, :], -1.0, None, ALU.mult))
                step(nc.vector.tensor_tensor(tmp, tmp, temp_s[:, :], ALU.min))
                dve.wait_ge(setup_act, 1)
                step(nc.vector.tensor_scalar(w, u, 1.0, None, ALU.add))
                dve.wait_ge(setup_act, 2)
                step(nc.vector.tensor_scalar(d, w, 1.0, None, ALU.subtract))
                step(nc.vector.tensor_scalar(e, d, 0.0, None, ALU.is_equal))
                step(nc.vector.tensor_tensor(d, d, e, ALU.add))
                step(nc.vector.tensor_tensor(ln_w, ln_w, e, ALU.add))
                step(nc.vector.reciprocal(d, d))
                step(nc.vector.tensor_tensor(d, d, ln_w, ALU.mult))
                step(nc.vector.tensor_tensor(d, d, u, ALU.mult))
                step(nc.vector.tensor_scalar(e, temp_s[:, :], 0.0, None, ALU.max))
                step(nc.vector.tensor_tensor(d, d, e, ALU.add))
                step(nc.vector.tensor_scalar(head_scale[:, :], d, float(D3) ** -0.5, None, ALU.mult))

            @block.scalar
            def _(act):
                act.wait_ge(setup_dve, 2)
                nc.scalar.activation(soft[:, 0, :], soft[:, 5, :], ACT.Exp).then_inc(setup_act, 1)
                act.wait_ge(setup_dve, 3)
                nc.scalar.activation(soft[:, 2, :], soft[:, 1, :], ACT.Ln).then_inc(setup_act, 1)
        nc.all_engine_barrier()

        def turn(b, more):
            with nc.Block() as block:
                @block.sync
                def _(sp):
                    if more:
                        sp.wait_ge(c_t_done, 1)
                        sp.dma_start(c_in[:, :, :], ctx_in[b + 1].rearrange("(t p) c -> p t c", p=P)).then_inc(c_loaded, 16)
                        sp.wait_ge(x_used, 1)
                        sp.dma_start(x_in[:, :, :], x[b + 1].rearrange("(t p) c -> p t c", p=P)).then_inc(x_loaded, 16)
                    sp.wait_ge(fq_t_done, 1)
                    for h in range(H3):
                        g = D3 * (h % HT)
                        sp.dma_start(fq_pad[g:g + D3, h, :], fq_t[g:g + D3, h // HT, :]).then_inc(fq_pad_done, 16)
                    sp.wait_ge(layer_done, 3)
                    sp.dma_start(out[b].rearrange("(t p) c -> p t c", p=P), out_s[:, :, :]).then_inc(out_stored, 16)
                    sp.wait_ge(fq_pad_done, 16 * H3)

                @block.gpsimd
                def _(pool):
                    for i in range(T * 2 * CHUNKS):
                        pool.wait_ge(halves_done, i + 1)
                        t, j = i // (2 * CHUNKS), i % (2 * CHUNKS)
                        nc.gpsimd.tensor_tensor(qk_rot[:, t, j * BANK:(j + 1) * BANK], rope_cos[:, i % 2, :],
                                                rope_sin[:, i % 2, :], ALU.add).then_inc(rot_done, 1)

                    def normalise(head):
                        n = INDEX[head]
                        pool.wait_ge(inv_done, n + 1)
                        widths = [(0, P), (P, 3 * P)] if head[0] == "self" else [(0, N), (N, 2 * N)]
                        for t, (lo, hi) in enumerate(widths):
                            tile = probs[:, n % P_SLOTS, lo:hi]
                            last = nc.gpsimd.tensor_scalar(tile, tile, row_inv[:, n, t:t + 1], 1.0, ALU.mult, ALU.mult)
                        last.then_inc(norm_done, 1)

                    steps = [0]

                    def inverse_std(n):
                        pool.wait_ge(moments_done, n + 1)
                        nc.gpsimd.tensor_scalar(var_eps[:, n, :], moments[:, n, :, 1], EPS, None, ALU.add).then_inc(pool_step, 1)
                        steps[0] += 1
                        pool.wait_ge(pool_step, steps[0])
                        nc.gpsimd.tensor_tensor(rstd[:, n, :], var_eps[:, n, :], power[:, 0:T], ALU.pow).then_inc(rstd_done, 1)

                    for h in range(H1):
                        normalise(("self", h))
                    inverse_std(0)
                    normalise(("cross", 0))
                    inverse_std(1)
                    pool.wait_ge(ss_done, 1)
                    nc.gpsimd.tensor_tensor(q_inv[:, :], q_ss[:, :], power[:, :], ALU.pow).then_inc(q_inv_done, 1)
                    for h in range(H3):
                        normalise(("moh", h))
                    inverse_std(2)

                @block.tensor
                def _(pe):
                    def transposed(item, src):
                        bank = lin.take(pe, item)
                        for k in range(KC):
                            for t in range(T):
                                last = nc.tensor.transpose(bank[:, k * N + t * P:k * N + (t + 1) * P],
                                                           src[:, t, k * P:(k + 1) * P], ident[:, :])
                        last.then_inc(lin.filled(item), 1)

                    def by_row(item, src_t, w, width):
                        bank = lin.take(pe, item)
                        for t in range(T):
                            for k in range(KC):
                                last = nc.tensor.matmul(bank[:, t * C:t * C + width], src_t[:, k, t * P:(t + 1) * P],
                                                        w[:, k, 0:width], start=(k == 0), stop=(k == KC - 1))
                        last.then_inc(lin.filled(item), 1)

                    def by_column(item, src_t, w):
                        bank = lin.take(pe, item)
                        for a in range(KC):
                            for k in range(KC):
                                last = nc.tensor.matmul(bank[:, a * N:(a + 1) * N], w[:, k, a * P:(a + 1) * P],
                                                        src_t[:, k, :], start=(k == 0), stop=(k == KC - 1))
                        last.then_inc(lin.filled(item), 1)

                    pe.wait_ge(x_loaded, (b + 1) * 16)
                    transposed("xT", x_in)
                    pe.wait_ge(c_loaded, (b + 1) * 16)
                    transposed("cT", c_in)
                    pe.wait_ge(x_t_done, 1)
                    for t in range(T):
                        for kind, n, base in (("qk", 2 * CHUNKS, 0), ("v", CHUNKS, 2 * E1)):
                            for j in range(n):
                                bank = lin.take(pe, (kind, t, j))
                                for k in range(KC):
                                    last = nc.tensor.matmul(bank[:, :], x_t[:, k, t * P:(t + 1) * P],
                                                            wqkv_s[:, k, base + j * BANK:base + (j + 1) * BANK],
                                                            start=(k == 0), stop=(k == KC - 1))
                                last.then_inc(lin.filled((kind, t, j)), 1)
                    pe.wait_ge(c_t_done, 1)
                    by_column("xk", c_t, square["xwk"])
                    by_row("xv", c_t, square["xwv"], C)

                    def pair_transposed(p):
                        pe.wait_ge(rot_done, 2 * CHUNKS + CHUNKS + p // 4 + 1)
                        bank = lin.take(pe, ("qkT", p))
                        for i in range(2):
                            for t in range(T):
                                last = nc.tensor.transpose(bank[:, i * N + t * P:i * N + (t + 1) * P],
                                                           qk_rot[:, t, i * E1 + p * P:i * E1 + (p + 1) * P], ident[:, :])
                        last.then_inc(lin.filled(("qkT", p)), 1)

                    def head_scores(head):
                        kind, h = head
                        if kind == "self":
                            p, slot = h // 2, (h // 2) % 2
                            pe.wait_ge(pair_done, p + 1)
                            bank = sc.take(pe, head)
                            nc.tensor.matmul(bank[:, 0:P], q_pad[:, slot, h % 2, 0:P], k_t[:, slot, 0:P],
                                             start=True, stop=True)
                            last = nc.tensor.matmul(bank[:, P:3 * P], q_pad[:, slot, h % 2, P:2 * P], k_t[:, slot, :],
                                                    start=True, stop=True)
                        elif kind == "cross":
                            pe.wait_ge(xk_done, 1)
                            pe.wait_ge(xq_done, 1)
                            bank = sc.take(pe, head)
                            for t in range(T):
                                for k in range(KC):
                                    last = nc.tensor.matmul(bank[:, t * N:(t + 1) * N], xq_t[:, k, t * P:(t + 1) * P],
                                                            xk_t[:, k, :], start=(k == 0), stop=(k == KC - 1))
                        else:
                            if h == 0:
                                pe.wait_ge(fk_done, 1)
                                pe.wait_ge(fq_pad_done, 16 * H3)
                            bank = sc.take(pe, head)
                            for t in range(T):
                                last = nc.tensor.matmul(bank[:, t * N:(t + 1) * N], fq_pad[:, h, t * P:(t + 1) * P],
                                                        fk_t[:, h // HT, :], start=True, stop=True)
                        last.then_inc(sc.filled(head), 1)

                    def head_transposed(head):
                        n = INDEX[head]
                        tile = probs[:, n % P_SLOTS, :]
                        pe.wait_ge(norm_done, n + 1)
                        bank = pt.take(pe, head)
                        if head[0] == "self":
                            blocks = [(0, 0), (P, P), (2 * P, 2 * P)]
                        else:
                            blocks = [(k * N + t * P, t * N + k * P) for k in range(T) for t in range(T)]
                        for dst, src in blocks:
                            last = nc.tensor.transpose(bank[:, dst:dst + P], tile[:, src:src + P], ident[:, :])
                        last.then_inc(pt.filled(head), 1)

                    def head_values(head):
                        kind, h = head
                        n = INDEX[head]
                        tile = probs_t[:, n % PT_SLOTS, :]
                        pe.wait_ge(probs_t_done, n + 1)
                        if kind == "self":
                            item = ("self", h // 2)
                            if h == 0:
                                pe.wait_ge(v1_done, T * CHUNKS)
                            bank = pv.take(pe, item) if h % 2 == 0 else pv.bank(item)
                            rows = bank[D1 * (h % 2):D1 * (h % 2) + D1, :]
                            nc.tensor.matmul(rows[:, 0:N], v1[:, 0, h * D1:(h + 1) * D1], tile[:, 0:N],
                                             start=True, stop=False)
                            last = nc.tensor.matmul(rows[:, P:N], v1[:, 1, h * D1:(h + 1) * D1], tile[:, N:N + P],
                                                    start=False, stop=True)
                        elif kind == "cross":
                            item = ("cross", 0)
                            pe.wait_ge(xv_done, 1)
                            bank = pv.take(pe, item)
                            for t in range(T):
                                for k in range(T):
                                    last = nc.tensor.matmul(bank[:, t * C:(t + 1) * C],
                                                            tile[:, k * N + t * P:k * N + (t + 1) * P], xv[:, k, :],
                                                            start=(k == 0), stop=(k == T - 1))
                        else:
                            item = ("moh", h // HT)
                            if h == 0:
                                pe.wait_ge(v_pad_done, 1)
                            bank = pv.take(pe, item) if h % HT == 0 else pv.bank(item)
                            for k in range(T):
                                last = nc.tensor.matmul(bank[:, 0:N], v_pad[:, k, h, :], tile[:, k * N:(k + 1) * N],
                                                        start=(h % HT == 0 and k == 0),
                                                        stop=(h % HT == HT - 1 and k == T - 1))
                        last.then_inc(head_done, 1)

                    def heads(todo, between=lambda i: None):
                        for i in range(len(todo) + LAG_PV):
                            if i < len(todo):
                                head_scores(todo[i])
                            between(i)
                            if 0 <= i - LAG_T < len(todo):
                                head_transposed(todo[i - LAG_T])
                            if 0 <= i - LAG_PV < len(todo):
                                head_values(todo[i - LAG_PV])

                    def next_pair(i):
                        if i % 2 == 1 and i // 2 + 2 < PAIRS:
                            pair_transposed(i // 2 + 2)

                    pair_transposed(0)
                    pair_transposed(1)
                    heads(HEADS[:H1], next_pair)

                    pe.wait_ge(o_t_done, PAIRS)
                    bank = lin.take(pe, "y")
                    for t in range(T):
                        for p in range(PAIRS):
                            last = nc.tensor.matmul(bank[:, t * C:(t + 1) * C], o_t[:, p, t * P:(t + 1) * P],
                                                    wout_s[:, p, :], start=(p == 0), stop=(p == PAIRS - 1))
                    last.then_inc(lin.filled("y"), 1)

                    pe.wait_ge(layer_done, 1)
                    transposed("x1T", x1)
                    pe.wait_ge(x1_t_done, 1)
                    by_column("xq", x1_t, square["xwq"])
                    heads(HEADS[H1:H1 + 1])

                    pe.wait_ge(layer_done, 2)
                    transposed("x2T", x2)
                    pe.wait_ge(x2_t_done, 1)
                    by_row("fq", x2_t, square["fwq"], C)
                    by_column("fk", x2_t, square["fwk"])
                    by_row("fv", x2_t, square["fwv"], C)
                    pe.wait_ge(fq_done, 1)
                    transposed("fqT", fq_f)
                    heads(HEADS[H1 + 1:])
                    pe.wait_ge(h_t_done, KC)
                    by_row("gate", h_t, gate_ws, NG)
                    by_row("ffn", h_t, square["fwp"], C)

                @block.scalar
                def _(act):
                    def copy(dst, item, done, src=None):
                        act.wait_ge(*lin.is_ready(item))
                        ins = nc.scalar.activation(dst, lin.bank(item)[:, :] if src is None else src, ACT.Copy)
                        ins.then_inc(done, 1)

                    def two(tile):
                        return tile[:, :, :].rearrange("p a n -> p (a n)")

                    copy(two(x_t), "xT", x_t_done)
                    copy(two(c_t), "cT", c_t_done)
                    for t in range(T):
                        for j in range(CHUNKS):
                            copy(v1[:, t, j * BANK:(j + 1) * BANK], ("v", t, j), v1_done)

                    def biased(dst, item, bias, done):
                        act.wait_ge(*lin.is_ready(item))
                        for a in range(KC):
                            last = nc.scalar.activation(dst[:, a, :], lin.bank(item)[:, a * N:(a + 1) * N],
                                                        ACT.Identity, bias=bias[:, a:a + 1])
                        last.then_inc(done, 1)

                    biased(xk_t, "xk", column["xbk"], xk_done)

                    def pair(p):
                        item, slot = ("qkT", p), p % 2
                        act.wait_ge(*lin.is_ready(item))
                        if p >= 2:
                            act.wait_ge(*sc.is_ready(("self", 2 * (p - 2) + 1)))
                            act.wait_ge(*sc.is_ready(("self", 2 * (p - 2))))
                        bank = lin.bank(item)
                        for i in range(2):
                            rows = slice(D1 * i, D1 * i + D1)
                            nc.scalar.activation(q_pad[rows, slot, i, :], bank[rows, 0:N], ACT.Copy)
                        nc.scalar.activation(k_t[:, slot, :], bank[:, N:2 * N], ACT.Copy)\
                            .then_inc(pair_done, 1)

                    def head_exp(head):
                        n = INDEX[head]
                        act.wait_ge(max_done, n + 1)
                        if n >= P_SLOTS:
                            act.wait_ge(*pt.is_ready(HEADS[n - P_SLOTS]))
                        if head[0] == "self":
                            parts = [(scores[:, n % S_SLOTS, lo:hi], lo, hi) for lo, hi in ((0, P), (P, 3 * P))]
                            sign = -1.0
                        else:
                            parts = [(sc.bank(head)[:, t * N:(t + 1) * N], t * N, (t + 1) * N) for t in range(T)]
                            sign = 1.0
                        for t, (src, lo, hi) in enumerate(parts):
                            last = nc.scalar.activation(probs[:, n % P_SLOTS, lo:hi], src, ACT.Exp,
                                                        bias=neg_max[:, n, t:t + 1], scale=sign,
                                                        accum_out=row_sum[:, n, t:t + 1])
                        last.then_inc(exp_done, 1)

                    def values(item, head, dst, done):
                        act.wait_ge(head_done, INDEX[head] + 1)
                        nc.scalar.activation(dst, pv.bank(item)[:, 0:N], ACT.Copy)\
                            .then_inc(done, 1)

                    pair(0)
                    pair(1)
                    for i in range(H1 + LAG_PV + 1):
                        if i < H1:
                            head_exp(("self", i))
                        if i % 2 == 1 and i // 2 + 2 < PAIRS:
                            pair(i // 2 + 2)
                        h = i - LAG_PV - 1
                        if h >= 0 and h % 2 == 1:
                            values(("self", h // 2), ("self", h), o_t[:, h // 2, :], o_t_done)
                    copy(two(x1_t), "x1T", x1_t_done)
                    head_exp(("cross", 0))
                    copy(two(x2_t), "x2T", x2_t_done)
                    biased(fk_t, "fk", column["fbk"], fk_done)
                    copy(two(fq_t), "fqT", fq_t_done)
                    for i in range(H3 + LAG_PV + 1):
                        if i < H3:
                            head_exp(("moh", i))
                        h = i - LAG_PV - 1
                        if h >= 0 and h % HT == HT - 1:
                            values(("moh", h // HT), ("moh", h), h_t[:, h // HT, :], h_t_done)
                    act.wait_ge(logits_done, 1)
                    nc.scalar.activation(gates[:, 2, :, :], gates[:, 1, :, :], ACT.Exp).then_inc(gate_exp_done, 1)

                @block.vector
                def _(dve):
                    count = [0]

                    def mark(ins):
                        count[0] += 1
                        return ins.then_inc(dve_step, 1)

                    def settled():
                        dve.wait_ge(dve_step, count[0])

                    for i in range(T * 2 * CHUNKS):
                        t, j = i // (2 * CHUNKS), i % (2 * CHUNKS)
                        which = j // CHUNKS
                        item = ("qk", t, j)
                        dve.wait_ge(*lin.is_ready(item))
                        if i >= 2:
                            dve.wait_ge(rot_done, i - 1)
                        bank = lin.bank(item)[:, :].rearrange("p (h s d) -> p h s d", s=2, d=D1 // 2)
                        shape = [P, BANK // D1, 2, D1 // 2]
                        cos = rope_s[:, t, which, 0, :].rearrange("p (o s d) -> p o s d", o=1, s=2).to_broadcast(shape)
                        sin = rope_s[:, t, which, 1, :].rearrange("p (o s d) -> p o s d", o=1, s=2).to_broadcast(shape)
                        dst = [r[:, i % 2, :].rearrange("p (h s d) -> p h s d", s=2, d=D1 // 2) for r in (rope_cos, rope_sin)]
                        nc.vector.tensor_tensor(dst[0], bank, cos, ALU.mult)
                        nc.vector.tensor_tensor(dst[1], bank[:, :, ::-1, :], sin, ALU.mult)\
                            .then_inc(halves_done, 1)

                    def plus_row(dst, item, bias):
                        dve.wait_ge(*lin.is_ready(item))
                        bank = lin.bank(item)[:, :].rearrange("p (t c) -> p t c", t=T)
                        wide = bias[:, :].rearrange("p (o c) -> p o c", o=1).to_broadcast([P, T, C])
                        return nc.vector.tensor_tensor(dst, bank, wide, ALU.add)

                    plus_row(xv[:, :, :], "xv", row["xbv"]).then_inc(xv_done, 1)

                    def head_max(head):
                        n = INDEX[head]
                        dve.wait_ge(*sc.is_ready(head))
                        bank = sc.bank(head)
                        if head[0] == "self":
                            if n >= S_SLOTS:
                                dve.wait_ge(exp_done, n - S_SLOTS + 1)
                            for t, (lo, hi) in enumerate(((0, P), (P, 3 * P))):
                                last = nc.vector.tensor_tensor_reduce(
                                    out=scores[:, n % S_SLOTS, lo:hi], in0=bank[:, lo:hi], in1=mask_s[:, lo:hi],
                                    scale=-1.0, scalar=3.4e38, op0=ALU.add, op1=ALU.min,
                                    accum_out=neg_max[:, n, t:t + 1])
                            last.then_inc(max_done, 1)
                        else:
                            nc.vector.tensor_reduce(neg_max[:, n, :], bank[:, :].rearrange("p (t n) -> p t n", t=T),
                                                    AX.X, ALU.max, negate=True).then_inc(max_done, 1)

                    def head_inverse(head):
                        n = INDEX[head]
                        dve.wait_ge(exp_done, n + 1)
                        nc.vector.reciprocal(row_inv[:, n, :], row_sum[:, n, :]).then_inc(inv_done, 1)

                    def head_evacuate(head):
                        n = INDEX[head]
                        width = 3 * P if head[0] == "self" else 2 * N
                        dve.wait_ge(*pt.is_ready(head))
                        if n >= PT_SLOTS:
                            dve.wait_ge(head_done, n - PT_SLOTS + 1)
                        nc.vector.tensor_copy(probs_t[:, n % PT_SLOTS, 0:width], pt.bank(head)[:, 0:width])\
                            .then_inc(probs_t_done, 1)

                    def heads(todo):
                        for i in range(len(todo) + LAG_PV):
                            if i < len(todo):
                                head_max(todo[i])
                            if 0 <= i - 1 < len(todo):
                                head_inverse(todo[i - 1])
                            if 0 <= i - LAG_T - 1 < len(todo):
                                head_evacuate(todo[i - LAG_T - 1])

                    def layernorm(n, dst):
                        settled()
                        for t in range(T):
                            mark(nc.vector.bn_stats(stats[:, n, t, :], z[:, n, t, :]))
                        settled()
                        for t in range(T):
                            last = nc.vector.bn_aggr(moments[:, n, t, :], stats[:, n, t, :])
                        last.then_inc(moments_done, 1)
                        dve.wait_ge(rstd_done, n + 1)
                        dve.wait_ge(moments_done, n + 1)
                        for t in range(T):
                            last = nc.vector.tensor_scalar(dst[:, t, :], z[:, n, t, :], moments[:, n, t, 0:1],
                                                           rstd[:, n, t:t + 1], ALU.subtract, ALU.mult)
                        last.then_inc(layer_done, 1)

                    def both(bank):
                        return bank[:, :].rearrange("p (t c) -> p t c", t=T)

                    heads(HEADS[:H1])
                    dve.wait_ge(*lin.is_ready("y"))
                    nc.vector.tensor_tensor(z[:, 0, :, :], both(lin.bank("y")), x_in[:, :, :], ALU.add)\
                        .then_inc(x_used, 1)
                    dve.wait_ge(x_used, 1)
                    layernorm(0, x1)

                    dve.wait_ge(*lin.is_ready("xq"))
                    for a in range(KC):
                        last = nc.vector.tensor_scalar(xq_t[:, a, :], lin.bank("xq")[:, a * N:(a + 1) * N],
                                                       column["xbq"][:, a:a + 1], float(C) ** -0.5, ALU.add, ALU.mult)
                    last.then_inc(xq_done, 1)
                    heads(HEADS[H1:H1 + 1])
                    dve.wait_ge(head_done, INDEX["cross", 0] + 1)
                    dve.wait_ge(layer_done, 1)
                    nc.vector.tensor_tensor(z[:, 1, :, :], both(pv.bank(("cross", 0))), x1[:, :, :], ALU.add)\
                        .then_inc(x1_used, 1)
                    dve.wait_ge(x1_used, 1)
                    layernorm(1, x2)

                    heads_of = "p t (h d) -> p t h d"
                    plus_row(fq[:, :, :], "fq", row["fbq"]).then_inc(fq_sum_done, 1)
                    dve.wait_ge(fq_sum_done, 1)
                    mark(nc.vector.tensor_tensor(fq_sq[:, :, :], fq[:, :, :], fq[:, :, :], ALU.mult))
                    settled()
                    nc.vector.tensor_reduce(q_ss[:, :], fq_sq[:, :, :].rearrange("p t (h d) -> p (t h) d", d=D3),
                                            AX.X, ALU.add).then_inc(ss_done, 1)
                    dve.wait_ge(*lin.is_ready("fv"))
                    for t in range(T):
                        for g in range(KC):
                            first = v_pad[:, t, g * HT, 0:D3]
                            src = lin.bank("fv")[:, t * C + g * P:t * C + (g + 1) * P]
                            bias = row["fbv"][:, g * P:(g + 1) * P]
                            last = nc.vector.tensor_tensor(diagonal(first), src.rearrange("p (h d) -> p h d", d=D3),
                                                           bias.rearrange("p (h d) -> p h d", d=D3), ALU.add)
                    last.then_inc(v_pad_done, 1)
                    dve.wait_ge(q_inv_done, 1)
                    shape = [P, T, H3, D3]
                    inv = q_inv[:, :].rearrange("p (t h o) -> p t h o", t=T, o=1).to_broadcast(shape)
                    mark(nc.vector.tensor_tensor(fq_n[:, :, :].rearrange(heads_of, h=H3), fq[:, :, :].rearrange(heads_of, h=H3),
                                                 inv, ALU.mult))
                    settled()
                    emb = row["qe"][:, :].rearrange("p (o c) -> p o c", o=1).to_broadcast([P, T, C])
                    mark(nc.vector.tensor_tensor(fq_e[:, :, :], fq_n[:, :, :], emb, ALU.add))
                    settled()
                    scale = head_scale[:, :].rearrange("p (u h o) -> p u h o", u=1, o=1).to_broadcast(shape)
                    nc.vector.tensor_tensor(fq_f[:, :, :].rearrange(heads_of, h=H3), fq_e[:, :, :].rearrange(heads_of, h=H3),
                                            scale, ALU.mult).then_inc(fq_done, 1)
                    heads(HEADS[H1 + 1:])

                    def small(i):
                        return gsmall[:, i, :]

                    def wide(i, n):
                        return gsmall[:, i, :].rearrange("p (t o) -> p t o", o=1).to_broadcast([P, T, n])

                    dve.wait_ge(*lin.is_ready("gate"))
                    bank = lin.bank("gate")[:, :].rearrange("p (t c) -> p t c", t=T)[:, :, 0:NG]
                    (nc.vector.tensor_tensor(gates[:, 0, :, :], bank,
                                                 gate_bs[:, :].rearrange("p (o c) -> p o c", o=1).to_broadcast([P, T, NG]),
                                                 ALU.add).then_inc(gate_sum_done, 1))
                    dve.wait_ge(gate_sum_done, 1)
                    routed, shared = slice(0, NR), slice(NR, NG)
                    mark(nc.vector.tensor_reduce(small(0), gates[:, 0, :, routed], AX.X, ALU.max))
                    mark(nc.vector.tensor_reduce(small(1), gates[:, 0, :, shared], AX.X, ALU.max))
                    settled()
                    nc.vector.tensor_tensor(gates[:, 1, :, routed], gates[:, 0, :, routed], wide(0, NR), ALU.subtract)
                    nc.vector.tensor_tensor(gates[:, 1, :, shared], gates[:, 0, :, shared], wide(1, NS), ALU.subtract)\
                        .then_inc(logits_done, 1)
                    dve.wait_ge(gate_exp_done, 1)
                    mark(nc.vector.tensor_reduce(small(2), gates[:, 2, :, routed], AX.X, ALU.add))
                    mark(nc.vector.tensor_reduce(small(3), gates[:, 2, :, shared], AX.X, ALU.add))
                    settled()
                    mark(nc.vector.reciprocal(gsmall[:, 4:6, :], gsmall[:, 2:4, :]))
                    settled()
                    mark(nc.vector.tensor_tensor(gates[:, 3, :, routed], gates[:, 2, :, routed], wide(4, NR), ALU.mult))
                    mark(nc.vector.tensor_tensor(gates[:, 3, :, shared], gates[:, 2, :, shared], wide(5, NS), ALU.mult))
                    settled()
                    for t in range(T):
                        mark(nc.vector.max(top8[:, t, :], gates[:, 3, t, routed]))
                    mark(nc.vector.tensor_reduce(small(6), gates[:, 3, :, shared], AX.X, ALU.add))
                    settled()
                    mark(nc.vector.tensor_reduce(small(7), top8[:, :, 0:TOPK], AX.X, ALU.add))
                    mark(nc.vector.tensor_tensor(small(8), gates[:, 3, :, NR], small(6), ALU.mult))
                    settled()
                    mark(nc.vector.scalar_tensor_tensor(small(9), small(7), float(TOPK), gates[:, 3, :, NR + 1], ALU.mult, ALU.mult))
                    settled()
                    mark(nc.vector.tensor_tensor(small(10), small(8), small(9), ALU.add))
                    settled()
                    mark(nc.vector.tensor_scalar(small(11), small(10), 2.0, None, ALU.mult))
                    settled()
                    dve.wait_ge(*lin.is_ready("ffn"))
                    dve.wait_ge(layer_done, 2)
                    for t in range(T):
                        mark(nc.vector.scalar_tensor_tensor(ffn[:, t, :], lin.bank("ffn")[:, t * C:(t + 1) * C],
                                                                  gsmall[:, 11, t:t + 1], x2[:, t, :], ALU.mult, ALU.add))
                    settled()
                    bias = row["fbp"][:, :].rearrange("p (o c) -> p o c", o=1).to_broadcast([P, T, C])
                    mark(nc.vector.tensor_tensor(z[:, 2, :, :], ffn[:, :, :], bias, ALU.add))
                    dve.wait_ge(out_stored, (b + 1) * 16)
                    layernorm(2, out_s)

            nc.all_engine_barrier(sems_to_clear=range(dve_step.num, pt.ready[-1].num + 1))

        with nc.Fori(0, B - 1) as b:
            turn(b, True)
        turn(B - 1, False)

        with nc.Block() as block:
            @block.sync
            def _(sp):
                sp.wait_ge(out_stored, 16 * (B + 1))


def diagonal(first):
    a = first.copy()
    return bass.AP(a.tensor, a.offset, [list(a.ap[0]), [P + D3, HT], [1, D3]])


def kernel(**inputs):
    import numpy as np
    import concourse.bacc as bacc
    from concourse.bass_utils import run_bass_kernel_spmd

    def arr(name):
        return np.asarray(inputs[name])

    f = np.float32
    inv_freq = (f(1.0) / np.power(f(10000.0), np.arange(0, D1, 2, dtype=f) / f(D1))).astype(f)
    angle = np.arange(N, dtype=f)[:, None] * inv_freq[None, :]
    cos, sin = np.cos(angle).astype(f), np.sin(angle).astype(f)
    table = np.stack([np.concatenate([cos, cos], 1), np.concatenate([-sin, sin], 1)], 1)
    table = np.stack([table * f(D1 ** -0.5), table], 1)
    rope = np.ascontiguousarray(table.reshape(T, P, 2, 2, D1).transpose(1, 0, 2, 3, 4))
    i, j = np.arange(P)[:, None], np.arange(P)[None, :]
    causal = np.where(j <= i, f(0), f(-BIG))
    band = np.where(j >= i, f(0), f(-BIG))
    mask = np.ascontiguousarray(np.concatenate([causal, band, causal], 1).astype(f))

    def cols(a):
        return a.reshape(KC, P).T

    arrays = {
        "x": arr("x"), "ctx_in": arr("ctx_1024"), "w_qkv": arr("L0_attn_W_qkv"), "w_out": arr("L0_attn_W_out"),
        "xwq": arr("L0_xattn_Wq"), "xbq": cols(arr("L0_xattn_bq")), "xwk": arr("L0_xattn_Wk"),
        "xbk": cols(arr("L0_xattn_bk")), "xwv": arr("L0_xattn_Wv"), "xbv": arr("L0_xattn_bv"),
        "fwq": arr("L0_ffn_Wq").T, "fbq": arr("L0_ffn_bq"), "fwk": arr("L0_ffn_Wk").T, "fbk": cols(arr("L0_ffn_bk")),
        "fwv": arr("L0_ffn_Wv").T, "fbv": arr("L0_ffn_bv"), "fwp": arr("L0_ffn_Wp").T, "fbp": arr("L0_ffn_bp"),
        "gate_w": np.concatenate([arr("L0_ffn_Wr"), arr("L0_ffn_Ws")], 0).T,
        "gate_b": np.concatenate([arr("L0_ffn_br"), arr("L0_ffn_bs")], 0),
        "temperature": arr("L0_ffn_temperature").reshape(-1),
        "query_embedding": arr("L0_ffn_query_embedding").reshape(-1),
        "rope": rope, "mask": mask, "identity": np.eye(P, dtype=f),
    }
    nc = bacc.Bacc("TRN2", target_bir_lowering=False, num_devices=1)
    given, args = {}, {}
    for name, a in arrays.items():
        a = np.ascontiguousarray(a)
        given[f"in_{name}"] = a
        args[name] = nc.dram_tensor(f"in_{name}", a.shape, mybir.dt.from_np(a.dtype), kind="ExternalInput").ap()
    args["out"] = nc.dram_tensor("out_0", (B, N, C), F32, kind="ExternalOutput").ap()
    decoder_layer(nc, **args)
    r = run_bass_kernel_spmd(nc, [given], core_ids=[0])
    return r.results[0]["out_0"]
```

```python
from contextlib import ExitStack

import concourse.bass as bass
from concourse import mybir

F32 = mybir.dt.float32
ALU = mybir.AluOpType
ACT = mybir.ActivationFunctionType
AX = mybir.AxisListType

P = 128
B = 16
N = 256
C = 256
T = N // P
KC = C // P
H1, D1 = 16, 64
E1 = H1 * D1
PAIRS = H1 // 2
H3, D3 = 16, 16
HT = P // D3
NR, NS = 15, 2
NG = NR + NS
TOPK = 3
BANK = 512
EPS = 1e-5
CHUNKS = E1 // BANK
BIG = 3.0e38

P_SLOTS, PT_SLOTS, S_SLOTS = 4, 3, 3
LEAD = 6
N_HEADS = H1 + 1 + H3


def turn_script(first, middle, last):
    script = ["xT"] * first + ["gate", "logits"] * last + ["x1T", "cT"] * middle
    qkv = []
    for t in range(T):
        qkv += [("qk", t, j) for j in range(2 * CHUNKS)] + [("v", t, j) for j in range(CHUNKS)]
    cross = ("cross", 0)
    between = [["xk", "xv", "xq"] * middle, ["factor"] * last, [("S", cross)] * middle, ["ffn", "sum3"] * last,
               [("I", cross), ("T", cross)] * middle, ["z3"] * last, [("V", cross), "z2"] * middle,
               ["norm3"] * last, ["norm2", "x2T"] * middle, ["fq", "fk", "fv"] * middle, ["fq_squares"] * middle, []]
    for unit, steps in zip(qkv, between):
        script += [unit] * first + steps
    own = [("self", h) for h in range(H1)] if first else []
    other = [("moh", h) for h in range(H3)] if middle else []
    order = own[:LEAD] if first else []
    for i in range(max(len(own) - LEAD, 0)):
        order += own[LEAD + i:LEAD + i + 1] + other[i:i + 1]
    order += other[max(len(own) - LEAD, 0):]
    if first:
        script += [("pair", 0), ("pair", 1)]
    heads = [cross] * middle + order
    after = {}
    if middle:
        at = min(1, len(own))
        after.setdefault(at if first else -1, []).append("fq_scaled")
        after.setdefault(at + 1 if first else -1, []).append("fqT")
    if first:
        ends = order.index(own[-1]) + 3
        for k, step in enumerate(("y", "z1", "norm1")):
            after.setdefault(ends + 1 + k, []).append(step)
    script += after.pop(-1, [])
    for i in range(max(len(order) + 3, max(after, default=0) + 1)):
        for name, lag in (("S", 0), ("I", 1), ("T", 2), ("V", 3)):
            if 0 <= i - lag < len(order):
                script.append((name, order[i - lag]))
            if name == "S" and i < len(order) and order[i][0] == "self":
                h = order[i][1]
                if h % 2 == 1 and h // 2 + 2 < PAIRS:
                    script.append(("pair", h // 2 + 2))
        script += after.get(i, [])
    return script, heads


class Ring:

    def __init__(self, banks, ready, order, read_out):
        self.banks, self.ready, self.order, self.read_out = banks, ready, order, read_out

    def bank(self, item):
        return self.banks[self.order.index(item) % len(self.banks)]

    def is_ready(self, item):
        n, r = self.order.index(item), len(self.banks)
        return self.ready[n % r], n // r + 1

    def filled(self, item):
        return self.ready[self.order.index(item) % len(self.banks)]

    def take(self, pe, item):
        n, r = self.order.index(item), len(self.banks)
        if n >= r:
            pe.wait_ge(*self.read_out[self.order[n - r]])
        return self.banks[n % r]


def decoder_layer(nc, x, ctx_in, w_qkv, w_out, xwq, xbq, xwk, xbk, xwv, xbv, fwq, fbq, fwk, fbk,
                  fwv, fbv, fwp, fbp, gate_w, gate_b, temperature, query_embedding,
                  rope, mask, identity, out):
    with ExitStack() as ctx:
        def sb(name, *shape):
            return ctx.enter_context(nc.sbuf_tensor(name, list(shape), F32))

        def sem(name):
            return ctx.enter_context(nc.semaphore(name))

        wqkv_s = sb("wqkv_s", P, KC, 3 * E1)
        wout_s = sb("wout_s", P, PAIRS, C)
        square = {n: sb(n + "_s", P, KC, C) for n in ("xwq", "xwk", "xwv", "fwq", "fwk", "fwv", "fwp")}
        gate_ws = sb("gate_ws", P, KC, NG)
        gate_bs = sb("gate_bs", P, NG)
        column = {n: sb(n + "_c", P, KC) for n in ("xbq", "xbk", "fbk")}
        row = {n: sb(n + "_r", P, C) for n in ("xbv", "fbq", "fbv", "fbp", "qe")}
        temp_s = sb("temp_s", P, H3)
        soft = sb("soft", P, 6, H3)
        head_scale = sb("head_scale", P, H3)
        rope_s = sb("rope_s", P, T, 2, 2, D1)
        mask_s = sb("mask_s", P, 3 * P)
        ident = sb("ident", P, P)
        power = sb("power", P, T * H3)

        x_in = sb("x_in", P, T, C)
        c_in = sb("c_in", P, T, C)
        x_t = sb("x_t", P, KC, N)
        c_t = sb("c_t", P, KC, N)
        rope_cos = sb("rope_cos", P, 2, BANK)
        rope_sin = sb("rope_sin", P, 2, BANK)
        qk_rot = sb("qk_rot", P, T, 2 * E1)
        v1 = sb("v1", P, T, E1)
        q_pad = sb("q_pad", P, 2, 2, N)
        k_t = sb("k_t", P, 2, N)
        scores = sb("scores", P, S_SLOTS, 3 * P)
        neg_max = sb("neg_max", P, N_HEADS, T)
        row_sum = sb("row_sum", P, N_HEADS, T)
        row_inv = sb("row_inv", P, N_HEADS, T)
        probs = sb("probs", P, P_SLOTS, T * N)
        probs_t = sb("probs_t", P, PT_SLOTS, T * N)
        o_t = sb("o_t", P, PAIRS, N)
        z = sb("z", P, 3, T, C)
        stats = sb("stats", P, 3, T, 6)
        moments = sb("moments", P, 3, T, 2)
        var_eps = sb("var_eps", P, 3, T)
        rstd = sb("rstd", P, 3, T)
        x1 = sb("x1", P, T, C)
        x1_t = sb("x1_t", P, KC, N)
        xq_t = sb("xq_t", P, KC, N)
        xk_t = sb("xk_t", P, KC, N)
        xv = sb("xv", P, T, C)
        x2 = sb("x2", P, T, C)
        x2_t = sb("x2_t", P, KC, N)
        fq = sb("fq", P, T, C)
        fq_sq = sb("fq_sq", P, T, C)
        fq_n = sb("fq_n", P, T, C)
        fq_e = sb("fq_e", P, T, C)
        fq_f = sb("fq_f", P, T, C)
        q_ss = sb("q_ss", P, T * H3)
        q_inv = sb("q_inv", P, T * H3)
        fq_t = sb("fq_t", P, KC, N)
        fk_t = sb("fk_t", P, KC, N)
        fq_pad = sb("fq_pad", P, H3, N)
        v_pad = sb("v_pad", P, T, H3, P)
        h_t = sb("h_t", P, KC, N)
        gates = sb("gates", P, 5, T, NG)
        gsmall = sb("gsmall", P, 12, T)
        top8 = sb("top8", P, T, 8)
        ffn = sb("ffn", P, T, C)
        out_s = sb("out_s", P, T, C)

        def banks(name, n):
            return [ctx.enter_context(nc.psum_tensor(f"{name}{i}", [P, BANK], F32)) for i in range(n)]

        lin_banks, sc_banks, pt_banks = banks("lin", 2), banks("sc", 2), banks("pt", 2)
        pv_self, pv_other = banks("pv", 2)

        w_loaded, x_loaded, c_loaded, out_stored = sem("w_loaded"), sem("x_loaded"), sem("c_loaded"), sem("out_stored")
        setup_dve, setup_act = sem("setup_dve"), sem("setup_act")

        dve_step = sem("dve_step")
        var_done = [sem(f"var_done{i}") for i in range(3)]
        x_t_done, c_t_done = sem("x_t_done"), sem("c_t_done")
        halves_done, rot_done = sem("halves_done"), sem("rot_done")
        v1_done, pair_done = sem("v1_done"), sem("pair_done")
        max_done, exp_done, inv_done, norm_done = sem("max_done"), sem("exp_done"), sem("inv_done"), sem("norm_done")
        probs_t_done, head_done = sem("probs_t_done"), sem("head_done")
        o_t_done = sem("o_t_done")
        moments_done = [sem(f"moments_done{i}") for i in range(3)]
        rstd_done = [sem(f"rstd_done{i}") for i in range(3)]
        layer_done = [sem(f"layer_done{i}") for i in range(3)]
        ffn_read = sem("ffn_read")
        x1_t_done, x2_t_done = sem("x1_t_done"), sem("x2_t_done")
        xk_done, xv_done, xq_done = sem("xk_done"), sem("xv_done"), sem("xq_done")
        ss_done, q_inv_done, fq_done, fq_t_done, fq_pad_done = (
            sem("ss_done"), sem("q_inv_done"), sem("fq_done"), sem("fq_t_done"), sem("fq_pad_done"))
        fk_done, v_pad_done, h_t_done = sem("fk_done"), sem("v_pad_done"), sem("h_t_done")
        logits_done, gate_exp_done = sem("logits_done"), sem("gate_exp_done")
        x_used = sem("x_used")
        fq_sum_done, gate_sum_done, x1_used = sem("fq_sum_done"), sem("gate_sum_done"), sem("x1_used")

        lin_ready, sc_ready, pt_ready = ([sem(f"{n}_ready{i}") for i in range(2)] for n in ("lin", "sc", "pt"))

        lin_read = {"xT": (x_t_done, 1), "cT": (c_t_done, 1), "xk": (xk_done, 1), "xv": (xv_done, 1),
                    "y": (x_used, 1), "x1T": (x1_t_done, 1), "xq": (xq_done, 1), "x2T": (x2_t_done, 1),
                    "fq": (fq_sum_done, 1), "fk": (fk_done, 1), "fv": (v_pad_done, 1), "fqT": (fq_t_done, 1),
                    "gate": (gate_sum_done, 1), "ffn": (ffn_read, 1)}
        for t in range(T):
            lin_read |= {("qk", t, j): (halves_done, t * 2 * CHUNKS + j + 1) for j in range(2 * CHUNKS)}
            lin_read |= {("v", t, j): (v1_done, t * CHUNKS + j + 1) for j in range(CHUNKS)}
        lin_read |= {("pair", p): (pair_done, p + 1) for p in range(PAIRS)}

        n_loads = 0
        with nc.Block() as block:
            @block.sync
            def _(sp):
                nonlocal n_loads
                loads = [(wqkv_s[:, :, :], w_qkv.rearrange("(k p) n -> p k n", p=P)),
                         (wout_s[:, :, :], w_out.rearrange("(k p) n -> p k n", p=P)),
                         (gate_ws[:, :, :], gate_w.rearrange("(k p) n -> p k n", p=P)),
                         (rope_s[:, :, :, :, :], rope), (mask_s[:, :], mask), (ident[:, :], identity)]
                for tile, w in zip(square.values(), (xwq, xwk, xwv, fwq, fwk, fwv, fwp)):
                    loads.append((tile[:, :, :], w.rearrange("(k p) n -> p k n", p=P)))
                for tile, v in zip(row.values(), (xbv, fbq, fbv, fbp, query_embedding)):
                    loads.append((tile[:, :], v.partition_broadcast(P)))
                loads.append((gate_bs[:, :], gate_b.partition_broadcast(P)))
                loads.append((temp_s[:, :], temperature.partition_broadcast(P)))
                for tile, v in zip(column.values(), (xbq, xbk, fbk)):
                    loads.append((tile[:, :], v))
                for dst, src in loads:
                    sp.dma_start(dst, src).then_inc(w_loaded, 16)
                n_loads = len(loads)
                sp.sem_inc(out_stored, 16)
                sp.dma_start(x_in[:, :, :], x[0].rearrange("(t p) c -> p t c", p=P)).then_inc(x_loaded, 16)
                sp.dma_start(c_in[:, :, :], ctx_in[0].rearrange("(t p) c -> p t c", p=P)).then_inc(c_loaded, 16)
                sp.wait_ge(w_loaded, 16 * n_loads)

            @block.vector
            def _(dve):
                for tile in (q_pad[:, :, :, :], fq_pad[:, :, :], v_pad[:, :, :, :]):
                    nc.vector.memset(tile, 0.0)
                nc.vector.memset(power[:, :], -0.5)
                count = [0]

                def step(ins):
                    count[0] += 1
                    ins.then_inc(setup_dve, 1)
                    dve.wait_ge(setup_dve, count[0])

                u, w, ln_w, d, e, tmp = (soft[:, i, :] for i in range(6))
                dve.wait_ge(w_loaded, 16 * n_loads)
                step(nc.vector.tensor_scalar(tmp, temp_s[:, :], -1.0, None, ALU.mult))
                step(nc.vector.tensor_tensor(tmp, tmp, temp_s[:, :], ALU.min))
                dve.wait_ge(setup_act, 1)
                step(nc.vector.tensor_scalar(w, u, 1.0, None, ALU.add))
                dve.wait_ge(setup_act, 2)
                step(nc.vector.tensor_scalar(d, w, 1.0, None, ALU.subtract))
                step(nc.vector.tensor_scalar(e, d, 0.0, None, ALU.is_equal))
                step(nc.vector.tensor_tensor(d, d, e, ALU.add))
                step(nc.vector.tensor_tensor(ln_w, ln_w, e, ALU.add))
                step(nc.vector.reciprocal(d, d))
                step(nc.vector.tensor_tensor(d, d, ln_w, ALU.mult))
                step(nc.vector.tensor_tensor(d, d, u, ALU.mult))
                step(nc.vector.tensor_scalar(e, temp_s[:, :], 0.0, None, ALU.max))
                step(nc.vector.tensor_tensor(d, d, e, ALU.add))
                step(nc.vector.tensor_scalar(head_scale[:, :], d, float(D3) ** -0.5, None, ALU.mult))

            @block.scalar
            def _(act):
                act.wait_ge(setup_dve, 2)
                nc.scalar.activation(soft[:, 0, :], soft[:, 5, :], ACT.Exp).then_inc(setup_act, 1)
                act.wait_ge(setup_dve, 3)
                nc.scalar.activation(soft[:, 2, :], soft[:, 1, :], ACT.Ln).then_inc(setup_act, 1)
        nc.all_engine_barrier()

        def turn(b, first, middle, last):
            script, heads = turn_script(first, middle, last)
            index = {head: n for n, head in enumerate(heads)}
            lin = Ring(lin_banks, lin_ready, [s for s in script if s in lin_read], lin_read)
            sc = Ring(sc_banks, sc_ready, heads, {h: (max_done if h[0] == "self" else exp_done, n + 1)
                                                  for n, h in enumerate(heads)})
            pt = Ring(pt_banks, pt_ready, heads, {h: (probs_t_done, n + 1) for n, h in enumerate(heads)})

            with nc.Block() as block:
                @block.sync
                def _(sp):
                    def load_next_context():
                        sp.wait_ge(c_t_done, 1)
                        sp.dma_start(c_in[:, :, :], ctx_in[b].rearrange("(t p) c -> p t c", p=P)).then_inc(c_loaded, 16)

                    def load_next_rows():
                        sp.wait_ge(x_used, 1)
                        sp.dma_start(x_in[:, :, :], x[b + 1].rearrange("(t p) c -> p t c", p=P)).then_inc(x_loaded, 16)

                    for step in script:
                        if step == "cT" and first:
                            load_next_context()
                        elif step == "norm3":
                            sp.wait_ge(layer_done[2], 1)
                            sp.dma_start(out[b - 2].rearrange("(t p) c -> p t c", p=P), out_s[:, :, :]).then_inc(out_stored, 16)
                        elif step == "fqT":
                            sp.wait_ge(fq_t_done, 1)
                            for h in range(H3):
                                g = D3 * (h % HT)
                                sp.dma_start(fq_pad[g:g + D3, h, :], fq_t[g:g + D3, h // HT, :]).then_inc(fq_pad_done, 16)
                        elif step == "z1" and not (isinstance(b, int) and b == B - 1):
                            load_next_rows()
                    if middle:
                        sp.wait_ge(fq_pad_done, 16 * H3)

                @block.gpsimd
                def _(pool):
                    def inverse_std(n):
                        pool.wait_ge(moments_done[n], 1)
                        nc.gpsimd.tensor_scalar(var_eps[:, n, :], moments[:, n, :, 1], EPS, None, ALU.add)\
                            .then_inc(var_done[n], 1)
                        pool.wait_ge(var_done[n], 1)
                        nc.gpsimd.tensor_tensor(rstd[:, n, :], var_eps[:, n, :], power[:, 0:T], ALU.pow)\
                            .then_inc(rstd_done[n], 1)

                    for step in script:
                        if step[0] == "qk":
                            _, t, j = step
                            i = t * 2 * CHUNKS + j
                            pool.wait_ge(halves_done, i + 1)
                            nc.gpsimd.tensor_tensor(qk_rot[:, t, j * BANK:(j + 1) * BANK], rope_cos[:, i % 2, :],
                                                    rope_sin[:, i % 2, :], ALU.add).then_inc(rot_done, 1)
                        elif step[0] == "I":
                            head = step[1]
                            n = index[head]
                            pool.wait_ge(inv_done, n + 1)
                            for t, (lo, hi) in enumerate([(0, P), (P, 3 * P)] if head[0] == "self" else [(0, N), (N, 2 * N)]):
                                tile = probs[:, n % P_SLOTS, lo:hi]
                                ins = nc.gpsimd.tensor_scalar(tile, tile, row_inv[:, n, t:t + 1], 1.0, ALU.mult, ALU.mult)
                            ins.then_inc(norm_done, 1)
                        elif step in ("z1", "z2", "z3"):
                            inverse_std(int(step[1]) - 1)
                        elif step == "fq_squares":
                            pool.wait_ge(ss_done, 1)
                            nc.gpsimd.tensor_tensor(q_inv[:, :], q_ss[:, :], power[:, :], ALU.pow).then_inc(q_inv_done, 1)

                @block.tensor
                def _(pe):
                    def transposed(item, src):
                        bank = lin.take(pe, item)
                        for k in range(KC):
                            for t in range(T):
                                ins = nc.tensor.transpose(bank[:, k * N + t * P:k * N + (t + 1) * P],
                                                          src[:, t, k * P:(k + 1) * P], ident[:, :])
                        ins.then_inc(lin.filled(item), 1)

                    def by_row(item, src_t, w, width):
                        bank = lin.take(pe, item)
                        for t in range(T):
                            for k in range(KC):
                                ins = nc.tensor.matmul(bank[:, t * C:t * C + width], src_t[:, k, t * P:(t + 1) * P],
                                                       w[:, k, 0:width], start=(k == 0), stop=(k == KC - 1))
                        ins.then_inc(lin.filled(item), 1)

                    def by_column(item, src_t, w):
                        bank = lin.take(pe, item)
                        for a in range(KC):
                            for k in range(KC):
                                ins = nc.tensor.matmul(bank[:, a * N:(a + 1) * N], w[:, k, a * P:(a + 1) * P],
                                                       src_t[:, k, :], start=(k == 0), stop=(k == KC - 1))
                        ins.then_inc(lin.filled(item), 1)

                    def head_scores(head):
                        kind, h = head
                        if kind == "self":
                            p, slot = h // 2, (h // 2) % 2
                            pe.wait_ge(pair_done, p + 1)
                            bank = sc.take(pe, head)
                            nc.tensor.matmul(bank[:, 0:P], q_pad[:, slot, h % 2, 0:P], k_t[:, slot, 0:P],
                                             start=True, stop=True)
                            ins = nc.tensor.matmul(bank[:, P:3 * P], q_pad[:, slot, h % 2, P:2 * P], k_t[:, slot, :],
                                                   start=True, stop=True)
                        elif kind == "cross":
                            pe.wait_ge(xk_done, 1)
                            pe.wait_ge(xq_done, 1)
                            bank = sc.take(pe, head)
                            for t in range(T):
                                for k in range(KC):
                                    ins = nc.tensor.matmul(bank[:, t * N:(t + 1) * N], xq_t[:, k, t * P:(t + 1) * P],
                                                           xk_t[:, k, :], start=(k == 0), stop=(k == KC - 1))
                        else:
                            if h == 0:
                                pe.wait_ge(fk_done, 1)
                                pe.wait_ge(fq_pad_done, 16 * H3)
                            bank = sc.take(pe, head)
                            for t in range(T):
                                ins = nc.tensor.matmul(bank[:, t * N:(t + 1) * N], fq_pad[:, h, t * P:(t + 1) * P],
                                                       fk_t[:, h // HT, :], start=True, stop=True)
                        ins.then_inc(sc.filled(head), 1)

                    def head_transposed(head):
                        n = index[head]
                        tile = probs[:, n % P_SLOTS, :]
                        pe.wait_ge(norm_done, n + 1)
                        bank = pt.take(pe, head)
                        if head[0] == "self":
                            blocks = [(0, 0), (P, P), (2 * P, 2 * P)]
                        else:
                            blocks = [(k * N + t * P, t * N + k * P) for k in range(T) for t in range(T)]
                        for dst, src in blocks:
                            ins = nc.tensor.transpose(bank[:, dst:dst + P], tile[:, src:src + P], ident[:, :])
                        ins.then_inc(pt.filled(head), 1)

                    def head_values(head):
                        kind, h = head
                        n = index[head]
                        tile = probs_t[:, n % PT_SLOTS, :]
                        pe.wait_ge(probs_t_done, n + 1)
                        if kind == "self":
                            if h == 0:
                                pe.wait_ge(v1_done, T * CHUNKS)
                            elif h % 2 == 0:
                                pe.wait_ge(o_t_done, h // 2)
                            rows = pv_self[D1 * (h % 2):D1 * (h % 2) + D1, :]
                            nc.tensor.matmul(rows[:, 0:N], v1[:, 0, h * D1:(h + 1) * D1], tile[:, 0:N],
                                             start=True, stop=False)
                            ins = nc.tensor.matmul(rows[:, P:N], v1[:, 1, h * D1:(h + 1) * D1], tile[:, N:N + P],
                                                   start=False, stop=True)
                        elif kind == "cross":
                            pe.wait_ge(xv_done, 1)
                            for t in range(T):
                                for k in range(T):
                                    ins = nc.tensor.matmul(pv_other[:, t * C:(t + 1) * C],
                                                           tile[:, k * N + t * P:k * N + (t + 1) * P], xv[:, k, :],
                                                           start=(k == 0), stop=(k == T - 1))
                        else:
                            if h == 0:
                                pe.wait_ge(v_pad_done, 1)
                                pe.wait_ge(x1_used, 1)
                            elif h == HT:
                                pe.wait_ge(h_t_done, 1)
                            for k in range(T):
                                ins = nc.tensor.matmul(pv_other[:, 0:N], v_pad[:, k, h, :], tile[:, k * N:(k + 1) * N],
                                                       start=(h % HT == 0 and k == 0),
                                                       stop=(h % HT == HT - 1 and k == T - 1))
                        ins.then_inc(head_done, 1)

                    for step in script:
                        if step == "xT":
                            pe.wait_ge(x_loaded, (b + 1) * 16)
                            transposed("xT", x_in)
                        elif step == "gate":
                            by_row("gate", h_t, gate_ws, NG)
                        elif step == "ffn":
                            by_row("ffn", h_t, square["fwp"], C)
                        elif step == "x1T":
                            transposed("x1T", x1)
                        elif step == "cT":
                            pe.wait_ge(c_loaded, b * 16)
                            transposed("cT", c_in)
                        elif step[0] in ("qk", "v"):
                            kind, t, j = step
                            base = j * BANK + (2 * E1 if kind == "v" else 0)
                            pe.wait_ge(x_t_done, 1)
                            bank = lin.take(pe, step)
                            for k in range(KC):
                                ins = nc.tensor.matmul(bank[:, :], x_t[:, k, t * P:(t + 1) * P],
                                                       wqkv_s[:, k, base:base + BANK], start=(k == 0), stop=(k == KC - 1))
                            ins.then_inc(lin.filled(step), 1)
                        elif step == "xk":
                            pe.wait_ge(c_t_done, 1)
                            by_column("xk", c_t, square["xwk"])
                        elif step == "xv":
                            by_row("xv", c_t, square["xwv"], C)
                        elif step == "xq":
                            pe.wait_ge(x1_t_done, 1)
                            by_column("xq", x1_t, square["xwq"])
                        elif step == "x2T":
                            pe.wait_ge(layer_done[1], 1)
                            transposed("x2T", x2)
                        elif step == "fq":
                            pe.wait_ge(x2_t_done, 1)
                            by_row("fq", x2_t, square["fwq"], C)
                        elif step == "fk":
                            by_column("fk", x2_t, square["fwk"])
                        elif step == "fv":
                            by_row("fv", x2_t, square["fwv"], C)
                        elif step == "fqT":
                            pe.wait_ge(fq_done, 1)
                            transposed("fqT", fq_f)
                        elif step[0] == "pair":
                            p = step[1]
                            pe.wait_ge(rot_done, 2 * CHUNKS + CHUNKS + p // 4 + 1)
                            bank = lin.take(pe, step)
                            for i in range(2):
                                for t in range(T):
                                    ins = nc.tensor.transpose(bank[:, i * N + t * P:i * N + (t + 1) * P],
                                                              qk_rot[:, t, i * E1 + p * P:i * E1 + (p + 1) * P], ident[:, :])
                            ins.then_inc(lin.filled(step), 1)
                        elif step == "y":
                            pe.wait_ge(o_t_done, PAIRS)
                            bank = lin.take(pe, "y")
                            for t in range(T):
                                for p in range(PAIRS):
                                    ins = nc.tensor.matmul(bank[:, t * C:(t + 1) * C], o_t[:, p, t * P:(t + 1) * P],
                                                           wout_s[:, p, :], start=(p == 0), stop=(p == PAIRS - 1))
                            ins.then_inc(lin.filled("y"), 1)
                        elif step[0] == "S":
                            head_scores(step[1])
                        elif step[0] == "T":
                            head_transposed(step[1])
                        elif step[0] == "V":
                            head_values(step[1])

                @block.scalar
                def _(act):
                    def copy(dst, item, done):
                        act.wait_ge(*lin.is_ready(item))
                        nc.scalar.activation(dst, lin.bank(item)[:, :], ACT.Copy).then_inc(done, 1)

                    def two(tile):
                        return tile[:, :, :].rearrange("p a n -> p (a n)")

                    def biased(dst, item, bias, done):
                        act.wait_ge(*lin.is_ready(item))
                        for a in range(KC):
                            ins = nc.scalar.activation(dst[:, a, :], lin.bank(item)[:, a * N:(a + 1) * N],
                                                       ACT.Identity, bias=bias[:, a:a + 1])
                        ins.then_inc(done, 1)

                    def pair(p):
                        item, slot = ("pair", p), p % 2
                        act.wait_ge(*lin.is_ready(item))
                        if p >= 2:
                            for h in (2 * (p - 2), 2 * (p - 2) + 1):
                                act.wait_ge(*sc.is_ready(("self", h)))
                        bank = lin.bank(item)
                        for i in range(2):
                            rows = slice(D1 * i, D1 * i + D1)
                            nc.scalar.activation(q_pad[rows, slot, i, :], bank[rows, 0:N], ACT.Copy)
                        nc.scalar.activation(k_t[:, slot, :], bank[:, N:2 * N], ACT.Copy).then_inc(pair_done, 1)

                    def head_exp(head):
                        n = index[head]
                        act.wait_ge(max_done, n + 1)
                        if n >= P_SLOTS:
                            act.wait_ge(*pt.is_ready(heads[n - P_SLOTS]))
                        if head[0] == "self":
                            parts = [(scores[:, n % S_SLOTS, lo:hi], lo, hi) for lo, hi in ((0, P), (P, 3 * P))]
                            sign = -1.0
                        else:
                            parts = [(sc.bank(head)[:, t * N:(t + 1) * N], t * N, (t + 1) * N) for t in range(T)]
                            sign = 1.0
                        for t, (src, lo, hi) in enumerate(parts):
                            ins = nc.scalar.activation(probs[:, n % P_SLOTS, lo:hi], src, ACT.Exp,
                                                       bias=neg_max[:, n, t:t + 1], scale=sign,
                                                       accum_out=row_sum[:, n, t:t + 1])
                        ins.then_inc(exp_done, 1)

                    for step in script:
                        if step == "xT":
                            copy(two(x_t), "xT", x_t_done)
                        elif step == "cT":
                            copy(two(c_t), "cT", c_t_done)
                        elif step == "x1T":
                            copy(two(x1_t), "x1T", x1_t_done)
                        elif step == "x2T":
                            copy(two(x2_t), "x2T", x2_t_done)
                        elif step == "fqT":
                            copy(two(fq_t), "fqT", fq_t_done)
                        elif step[0] == "v":
                            _, t, j = step
                            copy(v1[:, t, j * BANK:(j + 1) * BANK], step, v1_done)
                        elif step == "xk":
                            biased(xk_t, "xk", column["xbk"], xk_done)
                        elif step == "fk":
                            biased(fk_t, "fk", column["fbk"], fk_done)
                        elif step[0] == "pair":
                            pair(step[1])
                        elif step[0] == "S":
                            head_exp(step[1])
                        elif step == "logits":
                            act.wait_ge(logits_done, 1)
                            nc.scalar.activation(gates[:, 2, :, :], gates[:, 1, :, :], ACT.Exp).then_inc(gate_exp_done, 1)
                        elif step[0] == "V":
                            kind, h = step[1]
                            if kind == "self" and h % 2 == 1:
                                act.wait_ge(head_done, index[step[1]] + 1)
                                nc.scalar.activation(o_t[:, h // 2, :], pv_self[:, 0:N], ACT.Copy).then_inc(o_t_done, 1)
                            elif kind == "moh" and h % HT == HT - 1:
                                act.wait_ge(head_done, index[step[1]] + 1)
                                nc.scalar.activation(h_t[:, h // HT, :], pv_other[:, 0:N], ACT.Copy).then_inc(h_t_done, 1)

                @block.vector
                def _(dve):
                    count = [0]

                    def mark(ins):
                        count[0] += 1
                        return ins.then_inc(dve_step, 1)

                    def settled():
                        dve.wait_ge(dve_step, count[0])

                    def both(bank):
                        return bank[:, :].rearrange("p (t c) -> p t c", t=T)

                    def rows_of(r):
                        return r[:, :].rearrange("p (o c) -> p o c", o=1).to_broadcast([P, T, C])

                    def rotate(step):
                        _, t, j = step
                        i = t * 2 * CHUNKS + j
                        dve.wait_ge(*lin.is_ready(step))
                        if i >= 2:
                            dve.wait_ge(rot_done, i - 1)
                        bank = lin.bank(step)[:, :].rearrange("p (h s d) -> p h s d", s=2, d=D1 // 2)
                        shape = [P, BANK // D1, 2, D1 // 2]
                        cos, sin = (rope_s[:, t, j // CHUNKS, f, :].rearrange("p (o s d) -> p o s d", o=1, s=2).to_broadcast(shape)
                                    for f in range(2))
                        dst = [r[:, i % 2, :].rearrange("p (h s d) -> p h s d", s=2, d=D1 // 2) for r in (rope_cos, rope_sin)]
                        nc.vector.tensor_tensor(dst[0], bank, cos, ALU.mult)
                        nc.vector.tensor_tensor(dst[1], bank[:, :, ::-1, :], sin, ALU.mult).then_inc(halves_done, 1)

                    def head_max(head):
                        n = index[head]
                        dve.wait_ge(*sc.is_ready(head))
                        bank = sc.bank(head)
                        if head[0] == "self":
                            if n >= S_SLOTS:
                                dve.wait_ge(exp_done, n - S_SLOTS + 1)
                            for t, (lo, hi) in enumerate(((0, P), (P, 3 * P))):
                                ins = nc.vector.tensor_tensor_reduce(
                                    out=scores[:, n % S_SLOTS, lo:hi], in0=bank[:, lo:hi], in1=mask_s[:, lo:hi],
                                    scale=-1.0, scalar=3.4e38, op0=ALU.add, op1=ALU.min,
                                    accum_out=neg_max[:, n, t:t + 1])
                            ins.then_inc(max_done, 1)
                        else:
                            nc.vector.tensor_reduce(neg_max[:, n, :], bank[:, :].rearrange("p (t n) -> p t n", t=T),
                                                    AX.X, ALU.max, negate=True).then_inc(max_done, 1)

                    def head_evacuate(head):
                        n = index[head]
                        width = 3 * P if head[0] == "self" else 2 * N
                        dve.wait_ge(*pt.is_ready(head))
                        if n >= PT_SLOTS:
                            dve.wait_ge(head_done, n - PT_SLOTS + 1)
                        nc.vector.tensor_copy(probs_t[:, n % PT_SLOTS, 0:width], pt.bank(head)[:, 0:width])\
                            .then_inc(probs_t_done, 1)

                    def moments_of(n):
                        for t in range(T):
                            mark(nc.vector.bn_stats(stats[:, n, t, :], z[:, n, t, :]))
                        settled()
                        for t in range(T):
                            ins = nc.vector.bn_aggr(moments[:, n, t, :], stats[:, n, t, :])
                        ins.then_inc(moments_done[n], 1)

                    def normed(n, dst):
                        dve.wait_ge(moments_done[n], 1)
                        dve.wait_ge(rstd_done[n], 1)
                        for t in range(T):
                            ins = nc.vector.tensor_scalar(dst[:, t, :], z[:, n, t, :], moments[:, n, t, 0:1],
                                                          rstd[:, n, t:t + 1], ALU.subtract, ALU.mult)
                        ins.then_inc(layer_done[n], 1)

                    heads_of = "p t (h d) -> p t h d"
                    per_head = [P, T, H3, D3]

                    def squares():
                        dve.wait_ge(fq_sum_done, 1)
                        mark(nc.vector.tensor_tensor(fq_sq[:, :, :], fq[:, :, :], fq[:, :, :], ALU.mult))
                        settled()
                        nc.vector.tensor_reduce(q_ss[:, :], fq_sq[:, :, :].rearrange("p t (h d) -> p (t h) d", d=D3),
                                                AX.X, ALU.add).then_inc(ss_done, 1)

                    def scaled_queries():
                        dve.wait_ge(q_inv_done, 1)
                        inv = q_inv[:, :].rearrange("p (t h o) -> p t h o", t=T, o=1).to_broadcast(per_head)
                        mark(nc.vector.tensor_tensor(fq_n[:, :, :].rearrange(heads_of, h=H3),
                                                     fq[:, :, :].rearrange(heads_of, h=H3), inv, ALU.mult))
                        settled()
                        mark(nc.vector.tensor_tensor(fq_e[:, :, :], fq_n[:, :, :], rows_of(row["qe"]), ALU.add))
                        settled()
                        scale = head_scale[:, :].rearrange("p (u h o) -> p u h o", u=1, o=1).to_broadcast(per_head)
                        nc.vector.tensor_tensor(fq_f[:, :, :].rearrange(heads_of, h=H3),
                                                fq_e[:, :, :].rearrange(heads_of, h=H3), scale, ALU.mult).then_inc(fq_done, 1)

                    def padded_values():
                        dve.wait_ge(*lin.is_ready("fv"))
                        for t in range(T):
                            for g in range(KC):
                                first = v_pad[:, t, g * HT, 0:D3]
                                src = lin.bank("fv")[:, t * C + g * P:t * C + (g + 1) * P]
                                bias = row["fbv"][:, g * P:(g + 1) * P]
                                ins = nc.vector.tensor_tensor(diagonal(first), src.rearrange("p (h d) -> p h d", d=D3),
                                                              bias.rearrange("p (h d) -> p h d", d=D3), ALU.add)
                        ins.then_inc(v_pad_done, 1)

                    routed, shared = slice(0, NR), slice(NR, NG)

                    def small(i):
                        return gsmall[:, i, :]

                    def wide(i, n):
                        return gsmall[:, i, :].rearrange("p (t o) -> p t o", o=1).to_broadcast([P, T, n])

                    def gate_logits():
                        dve.wait_ge(*lin.is_ready("gate"))
                        nc.vector.tensor_tensor(gates[:, 0, :, :], both(lin.bank("gate"))[:, :, 0:NG],
                                                gate_bs[:, :].rearrange("p (o c) -> p o c", o=1).to_broadcast([P, T, NG]),
                                                ALU.add).then_inc(gate_sum_done, 1)
                        dve.wait_ge(gate_sum_done, 1)
                        mark(nc.vector.tensor_reduce(small(0), gates[:, 0, :, routed], AX.X, ALU.max))
                        mark(nc.vector.tensor_reduce(small(1), gates[:, 0, :, shared], AX.X, ALU.max))
                        settled()
                        nc.vector.tensor_tensor(gates[:, 1, :, routed], gates[:, 0, :, routed], wide(0, NR), ALU.subtract)
                        nc.vector.tensor_tensor(gates[:, 1, :, shared], gates[:, 0, :, shared], wide(1, NS), ALU.subtract)\
                            .then_inc(logits_done, 1)

                    def gate_factor():
                        dve.wait_ge(gate_exp_done, 1)
                        mark(nc.vector.tensor_reduce(small(2), gates[:, 2, :, routed], AX.X, ALU.add))
                        mark(nc.vector.tensor_reduce(small(3), gates[:, 2, :, shared], AX.X, ALU.add))
                        settled()
                        mark(nc.vector.reciprocal(gsmall[:, 4:6, :], gsmall[:, 2:4, :]))
                        settled()
                        mark(nc.vector.tensor_tensor(gates[:, 3, :, routed], gates[:, 2, :, routed], wide(4, NR), ALU.mult))
                        mark(nc.vector.tensor_tensor(gates[:, 3, :, shared], gates[:, 2, :, shared], wide(5, NS), ALU.mult))
                        settled()
                        for t in range(T):
                            mark(nc.vector.max(top8[:, t, :], gates[:, 3, t, routed]))
                        mark(nc.vector.tensor_reduce(small(6), gates[:, 3, :, shared], AX.X, ALU.add))
                        settled()
                        mark(nc.vector.tensor_reduce(small(7), top8[:, :, 0:TOPK], AX.X, ALU.add))
                        mark(nc.vector.tensor_tensor(small(8), gates[:, 3, :, NR], small(6), ALU.mult))
                        settled()
                        mark(nc.vector.scalar_tensor_tensor(small(9), small(7), float(TOPK), gates[:, 3, :, NR + 1],
                                                            ALU.mult, ALU.mult))
                        settled()
                        mark(nc.vector.tensor_tensor(small(10), small(8), small(9), ALU.add))
                        settled()
                        mark(nc.vector.tensor_scalar(small(11), small(10), 2.0, None, ALU.mult))

                    def scaled_projection():
                        settled()
                        dve.wait_ge(*lin.is_ready("ffn"))
                        for t in range(T):
                            ins = nc.vector.scalar_tensor_tensor(ffn[:, t, :], lin.bank("ffn")[:, t * C:(t + 1) * C],
                                                                 gsmall[:, 11, t:t + 1], x2[:, t, :], ALU.mult, ALU.add)
                        ins.then_inc(ffn_read, 1)

                    for step in script:
                        if step[0] == "qk":
                            rotate(step)
                        elif step == "xv":
                            dve.wait_ge(*lin.is_ready("xv"))
                            nc.vector.tensor_tensor(xv[:, :, :], both(lin.bank("xv")), rows_of(row["xbv"]), ALU.add)\
                                .then_inc(xv_done, 1)
                        elif step == "xq":
                            dve.wait_ge(*lin.is_ready("xq"))
                            for a in range(KC):
                                ins = nc.vector.tensor_scalar(xq_t[:, a, :], lin.bank("xq")[:, a * N:(a + 1) * N],
                                                              column["xbq"][:, a:a + 1], float(C) ** -0.5, ALU.add, ALU.mult)
                            ins.then_inc(xq_done, 1)
                        elif step == "logits":
                            gate_logits()
                        elif step == "factor":
                            gate_factor()
                        elif step == "sum3":
                            scaled_projection()
                        elif step == "z1":
                            dve.wait_ge(*lin.is_ready("y"))
                            nc.vector.tensor_tensor(z[:, 0, :, :], both(lin.bank("y")), x_in[:, :, :], ALU.add)\
                                .then_inc(x_used, 1)
                            dve.wait_ge(x_used, 1)
                            moments_of(0)
                        elif step == "z2":
                            dve.wait_ge(head_done, index["cross", 0] + 1)
                            nc.vector.tensor_tensor(z[:, 1, :, :], both(pv_other), x1[:, :, :], ALU.add).then_inc(x1_used, 1)
                            dve.wait_ge(x1_used, 1)
                            moments_of(1)
                        elif step == "z3":
                            dve.wait_ge(ffn_read, 1)
                            mark(nc.vector.tensor_tensor(z[:, 2, :, :], ffn[:, :, :], rows_of(row["fbp"]), ALU.add))
                            settled()
                            moments_of(2)
                        elif step == "norm1":
                            normed(0, x1)
                        elif step == "norm2":
                            normed(1, x2)
                        elif step == "norm3":
                            dve.wait_ge(out_stored, (b - 1) * 16)
                            normed(2, out_s)
                        elif step == "fq":
                            dve.wait_ge(*lin.is_ready("fq"))
                            nc.vector.tensor_tensor(fq[:, :, :], both(lin.bank("fq")), rows_of(row["fbq"]), ALU.add)\
                                .then_inc(fq_sum_done, 1)
                        elif step == "fv":
                            padded_values()
                        elif step == "fq_squares":
                            squares()
                        elif step == "fq_scaled":
                            scaled_queries()
                        elif step[0] == "S":
                            head_max(step[1])
                        elif step[0] == "I":
                            n = index[step[1]]
                            dve.wait_ge(exp_done, n + 1)
                            nc.vector.reciprocal(row_inv[:, n, :], row_sum[:, n, :]).then_inc(inv_done, 1)
                        elif step[0] == "T":
                            head_evacuate(step[1])

            nc.all_engine_barrier(sems_to_clear=range(dve_step.num, pt_ready[-1].num + 1))

        turn(0, True, False, False)
        turn(1, True, True, False)
        with nc.Fori(2, B - 1) as b:
            turn(b, True, True, True)
        turn(B - 1, True, True, True)
        turn(B, False, True, True)
        turn(B + 1, False, False, True)

        with nc.Block() as block:
            @block.sync
            def _(sp):
                sp.wait_ge(out_stored, 16 * (B + 1))


def diagonal(first):
    a = first.copy()
    return bass.AP(a.tensor, a.offset, [list(a.ap[0]), [P + D3, HT], [1, D3]])


def kernel(**inputs):
    import numpy as np
    import concourse.bacc as bacc
    from concourse.bass_utils import run_bass_kernel_spmd

    def arr(name):
        return np.asarray(inputs[name])

    f = np.float32
    inv_freq = (f(1.0) / np.power(f(10000.0), np.arange(0, D1, 2, dtype=f) / f(D1))).astype(f)
    angle = np.arange(N, dtype=f)[:, None] * inv_freq[None, :]
    cos, sin = np.cos(angle).astype(f), np.sin(angle).astype(f)
    table = np.stack([np.concatenate([cos, cos], 1), np.concatenate([-sin, sin], 1)], 1)
    table = np.stack([table * f(D1 ** -0.5), table], 1)
    rope = np.ascontiguousarray(table.reshape(T, P, 2, 2, D1).transpose(1, 0, 2, 3, 4))
    i, j = np.arange(P)[:, None], np.arange(P)[None, :]
    causal = np.where(j <= i, f(0), f(-BIG))
    band = np.where(j >= i, f(0), f(-BIG))
    mask = np.ascontiguousarray(np.concatenate([causal, band, causal], 1).astype(f))

    def cols(a):
        return a.reshape(KC, P).T

    arrays = {
        "x": arr("x"), "ctx_in": arr("ctx_1024"), "w_qkv": arr("L0_attn_W_qkv"), "w_out": arr("L0_attn_W_out"),
        "xwq": arr("L0_xattn_Wq"), "xbq": cols(arr("L0_xattn_bq")), "xwk": arr("L0_xattn_Wk"),
        "xbk": cols(arr("L0_xattn_bk")), "xwv": arr("L0_xattn_Wv"), "xbv": arr("L0_xattn_bv"),
        "fwq": arr("L0_ffn_Wq").T, "fbq": arr("L0_ffn_bq"), "fwk": arr("L0_ffn_Wk").T, "fbk": cols(arr("L0_ffn_bk")),
        "fwv": arr("L0_ffn_Wv").T, "fbv": arr("L0_ffn_bv"), "fwp": arr("L0_ffn_Wp").T, "fbp": arr("L0_ffn_bp"),
        "gate_w": np.concatenate([arr("L0_ffn_Wr"), arr("L0_ffn_Ws")], 0).T,
        "gate_b": np.concatenate([arr("L0_ffn_br"), arr("L0_ffn_bs")], 0),
        "temperature": arr("L0_ffn_temperature").reshape(-1),
        "query_embedding": arr("L0_ffn_query_embedding").reshape(-1),
        "rope": rope, "mask": mask, "identity": np.eye(P, dtype=f),
    }
    nc = bacc.Bacc("TRN2", target_bir_lowering=False, num_devices=1)
    given, args = {}, {}
    for name, a in arrays.items():
        a = np.ascontiguousarray(a)
        given[f"in_{name}"] = a
        args[name] = nc.dram_tensor(f"in_{name}", a.shape, mybir.dt.from_np(a.dtype), kind="ExternalInput").ap()
    args["out"] = nc.dram_tensor("out_0", (B, N, C), F32, kind="ExternalOutput").ap()
    decoder_layer(nc, **args)
    r = run_bass_kernel_spmd(nc, [given], core_ids=[0])
    return r.results[0]["out_0"]
```

```python
from contextlib import ExitStack

import concourse.bass as bass
from concourse import mybir

F32 = mybir.dt.float32
F16 = mybir.dt.float16
BF16 = mybir.dt.bfloat16
F32R = mybir.dt.float32r
ALU = mybir.AluOpType
ACT = mybir.ActivationFunctionType
AX = mybir.AxisListType

P = 128
B = 16
N = 256
C = 256
T = N // P
KC = C // P
H1, D1 = 16, 64
E1 = H1 * D1
PAIRS = H1 // 2
H3, D3 = 16, 16
HT = P // D3
NR, NS = 15, 2
NG = NR + NS
TOPK = 3
BANK = 512
EPS = 1e-5
CHUNKS = E1 // BANK
BIG = 3.0e38

PARTS = 3
VW = PARTS * D3 + 1
GH = 4
P_SCALE = 4096.0
P_SLOTS, PT_SLOTS, S_SLOTS, HL_SLOTS = 5, 3, 3, 3
N_HEADS = H1 + 1 + H3
SPLIT_PRODUCTS = ((0, 0), (0, 1), (1, 0))
N_STACKED = 3 * HT



def head_of(m):
    return m // KC + m % KC * HT


def head_rows(m):
    return slice(P // 2 * (m // KC % 2), P // 2 * (m // KC % 2) + 3 * D3)


def head_slot(m):
    return m // KC // 2 * KC + m % KC


def group_column(m):
    return m % KC * (GH // KC) + m // KC % (GH // KC)


LAG = {"G": 7, "O": 7, "E": 5, "S": 0, "T": 4, "L": 2, "I": 1, "V": 6}
CROSS_TICK = 6
EARLY = (1, 4, 7, 9, 11)
BETWEEN = 6
POW_COLUMNS = 4
POW_STEPS = T * H3 // POW_COLUMNS


def turn_script(first, middle, attend, last):
    units = [(kind, t, j) for t in range(T) for kind, n in (("qk", 2 * CHUNKS), ("v", CHUNKS)) for j in range(n)]
    own = [("self", h) for h in range(H1)] if first else []
    other = [("moh", m) for m in range(H3)] if attend else []
    if first:
        starts = [None] * len(units)
        for tick in EARLY:
            starts[tick], other = (other or [None])[0], other[1:]
        for i, h in enumerate(own):
            take = i < BETWEEN or i % 2 == 1
            starts += [h] + other[:take]
            other = other[take:]
        starts += other
    else:
        starts = other
    if middle:
        if first:
            starts[CROSS_TICK] = ("cross", 0)
        else:
            starts.insert(CROSS_TICK, ("cross", 0))
    heads = [h for h in starts if h]

    at = {}

    def put(tick, *steps):
        at.setdefault(tick, []).extend(steps)

    if middle:
        put(0, "y")
        put(1, "y_rest", "z1")
        put(2, "xk")
        put(3, "norm1", "xv")
        put(4, "x1T")
        put(5, "xq")
        values = CROSS_TICK + LAG["V"]
        put(values, "z2")
        if attend:
            put(values - 2, "keep")
        put(values + 2, "norm2")
        put(values + 3, "x2T")
        put(values + 4, "fq")
        put(values + 5, "fk", "fq_squares")
        put(values + 6, "fv")
        for i in range(POW_STEPS):
            put(values + 6 + i, ("power", i))
        put(values + 7 + POW_STEPS, "fq_scaled")
        put(values + 8 + POW_STEPS, "fqT")
        for g in range(HT):
            free = starts.index(("moh", KC * g + KC - 1)) if attend else 0
            put(max(free + 1, values + 6), ("stack_k", g))
            put(max(free + 1, values + 9 + POW_STEPS), ("stack_q", g))
    elif attend:
        put(6, "keep")
    if attend:
        put(0, "parts_of_v")
    if last:
        put(1, "gate", "logits")
        put(4, "factor", "ffn", "sum3", "z3")
        put(7, "norm3")
    if first:
        for tick, unit in enumerate(units):
            put(tick, unit)
        put(len(units) - 1, ("pair", 0), ("pair_out", 0), ("pair", 1), ("pair_out", 1))
        copies = {}
        for p in range(2, PAIRS):
            tick = starts.index(("self", 2 * p - 3))
            put(tick, ("pair", p))
            copies[tick + 1] = [("pair_out", p)]

    if not first:
        copies = {}
    script = ["xT"] * first + ["hT"] * last + ["cT"] * middle
    for tick in range(max(max(at) + 1, len(starts) + LAG["G"] if starts else 0)):
        script += copies.get(tick, [])
        for name, lag in LAG.items():
            if 0 <= tick - lag < len(starts) and starts[tick - lag]:
                script.append((name, starts[tick - lag]))
        script += at.get(tick, [])
    return script, heads


LIN_STEPS = {("V", ("cross", 0)): "cross_values"}


class Ring:

    def __init__(self, banks, ready, order, read_out):
        self.banks, self.ready, self.order, self.read_out = banks, ready, order, read_out

    def bank(self, item):
        return self.banks[self.order.index(item) % len(self.banks)]

    def is_ready(self, item):
        n, r = self.order.index(item), len(self.banks)
        return self.ready[n % r], n // r + 1

    def filled(self, item):
        return self.ready[self.order.index(item) % len(self.banks)]

    def take(self, pe, item):
        n, r = self.order.index(item), len(self.banks)
        if n >= r:
            pe.wait_ge(*self.read_out[self.order[n - r]])
        return self.banks[n % r]


def decoder_layer(nc, x, ctx_in, w_qkv, w_out, xwq, xbq, xwk, xbk, xwv, xbv, fwq, fbq, fwk, fbk,
                  fwv, fbv, fwp, fbp, gate_w, gate_b, temperature, query_embedding,
                  rope, mask, identity, out):
    with ExitStack() as ctx:
        def sb(name, *shape, dtype=F32):
            return ctx.enter_context(nc.sbuf_tensor(name, list(shape), dtype))

        def sem(name):
            return ctx.enter_context(nc.semaphore(name))

        wqkv_high, wqkv_low = (sb(n, P, KC, 3 * E1, dtype=F32R) for n in ("wqkv_high", "wqkv_low"))
        wout_s = sb("wout_s", P, PAIRS, C)
        square = {n: sb(n + "_s", P, KC, C) for n in ("xwq", "xwk", "xwv", "fwq", "fwk", "fwv", "fwp")}
        gate_ws = sb("gate_ws", P, KC, NG)
        gate_bs = sb("gate_bs", P, NG)
        column = {n: sb(n + "_c", P, KC) for n in ("xbq", "xbk", "fbk")}
        row = {n: sb(n + "_r", P, C) for n in ("xbv", "fbq", "fbv", "fbp", "qe")}
        temp_s = sb("temp_s", P, H3)
        soft = sb("soft", P, 6, H3)
        head_scale = sb("head_scale", P, H3)
        rope_s = sb("rope_s", P, T, 2, 2, D1)
        mask_s = sb("mask_s", P, 3 * P)
        ident = sb("ident", P, P)
        power = sb("power", P, T * H3)

        x_in = sb("x_in", P, T, C)
        x_again = sb("x_again", P, T, C)
        c_in = sb("c_in", P, T, C)
        shared_high, shared_low = (sb(n, P, KC, N, dtype=F32R) for n in ("shared_high", "shared_low"))
        x_t_high, x_t_low = fk_high, fk_low = shared_high, shared_low
        c_t = xq_t = sb("c_t_xq_t", P, KC, N)
        fq_high, fq_low = (sb(n, P, KC, N, dtype=F32R) for n in ("fq_high", "fq_low"))
        rope_sin = [tile[:, :, :].rearrange("p k n -> p (k n)").bitcast(F32) for tile in (fq_high, fq_low)]
        qk_rot = sb("qk_rot", P, T, 2 * E1)
        v1 = sb("v1", P, T, E1)
        qk_t = sb("qk_t", P, 2, 2, N)
        scores = sb("scores", P, S_SLOTS, 3 * P)
        neg_max = sb("neg_max", P, N_HEADS, T)
        row_sum = sb("row_sum", P, N_HEADS, T)
        row_inv = sb("row_inv", P, N_HEADS, T)
        probs = sb("probs", P, P_SLOTS, T * N)
        probs_t = sb("probs_t", P, PT_SLOTS, T * N)
        o_t = sb("o_t", P, PAIRS, N)
        z = sb("z", P, 3, T, C)
        stats = sb("stats", P, 3, T, 6)
        moments = sb("moments", P, 3, T, 2)
        var_eps = sb("var_eps", P, 3, T)
        rstd = sb("rstd", P, 3, T)
        x1, x2, out_s = (z[:, n, :, :] for n in range(3))
        x1_t = sb("x1_t", P, KC, N)
        xk_t = sb("xk_t", P, KC, N)
        xv = sb("xv", P, T, C)
        x2_kept = sb("x2_kept", P, T, C)
        h_t = x2_t = sb("h_t_x2_t", P, KC, N)
        fq = sb("fq", P, T, C)
        q_ss = sb("q_ss", P, T * H3)
        q_inv = sb("q_inv", P, T * H3)
        fq_parts = sb("fq_parts", P, H3 // 2, N, dtype=F32R)
        fk_parts = sb("fk_parts", P, H3 // 2, N, dtype=F32R)
        fv = sb("fv", P, T, C)
        fv_rest = sb("fv_rest", P, T, C)
        v_parts = sb("v_parts", P, T, H3, VW, dtype=BF16)
        p_high = sb("p_high", P, HL_SLOTS, T * N, dtype=F16)
        p_low = sb("p_low", P, HL_SLOTS, T * N, dtype=F16)
        ident16 = sb("ident16", P, P, dtype=F16)
        h_sum = sb("h_sum", P, T * GH, D3)
        h_inv = sb("h_inv", P, T * GH)
        h_rows = sb("h_rows", P, T, C)
        gates = sb("gates", P, 5, T, NG)
        gsmall = sb("gsmall", P, 12, T)
        top8 = sb("top8", P, T, 8)

        def banks(name, n):
            return [ctx.enter_context(nc.psum_tensor(f"{name}{i}", [P, BANK], F32)) for i in range(n)]

        lin_banks, sc_banks, pt_banks = banks("lin", 2), banks("sc", 2), banks("pt", 2)
        pv_self, pv_other = banks("pv", 2)

        w_qkv_loaded, tables_loaded = sem("w_qkv_loaded"), sem("tables_loaded")
        w_loaded, x_loaded, c_loaded, out_stored = sem("w_loaded"), sem("x_loaded"), sem("c_loaded"), sem("out_stored")
        x_again_loaded = sem("x_again_loaded")
        setup_dve, setup_act, setup_high = sem("setup_dve"), sem("setup_act"), sem("setup_high")

        dve_step = sem("dve_step")
        var_done = [sem(f"var_done{i}") for i in range(3)]
        x_high_done, x_t_done, c_t_done = sem("x_high_done"), sem("x_t_done"), sem("c_t_done")
        halves_done, rot_done = sem("halves_done"), sem("rot_done")
        v1_done, pair_done = sem("v1_done"), sem("pair_done")
        max_done, exp_done, inv_done, norm_done = sem("max_done"), sem("exp_done"), sem("inv_done"), sem("norm_done")
        probs_t_done, head_done = sem("probs_t_done"), sem("head_done")
        o_t_done = sem("o_t_done")
        moments_done = [sem(f"moments_done{i}") for i in range(3)]
        rstd_done = [sem(f"rstd_done{i}") for i in range(3)]
        layer_done = [sem(f"layer_done{i}") for i in range(3)]
        ffn_read = sem("ffn_read")
        x1_t_done, x2_t_done = sem("x1_t_done"), sem("x2_t_done")
        xk_done, xv_done, xq_done = sem("xk_done"), sem("xv_done"), sem("xq_done")
        ss_done, q_inv_done, fq_done = sem("ss_done"), sem("q_inv_done"), sem("fq_done")
        fq_high_done, fq_low_done, fq_parts_done = sem("fq_high_done"), sem("fq_low_done"), sem("fq_parts_done")
        fk_high_done, fk_low_done, fk_parts_done = sem("fk_high_done"), sem("fk_low_done"), sem("fk_parts_done")
        fv_done, v_high_done, v_rest_done, v_mid_done, v_parts_done = (
            sem("fv_done"), sem("v_high_done"), sem("v_rest_done"), sem("v_mid_done"), sem("v_parts_done"))
        p_high_done, p_low_done, p_parts_t_done = sem("p_high_done"), sem("p_low_done"), sem("p_parts_t_done")
        h_read, h_rows_done, h_t_done = sem("h_read"), sem("h_rows_done"), sem("h_t_done")
        logits_done, gate_exp_done = sem("logits_done"), sem("gate_exp_done")
        x_used, x2_kept_done = sem("x_used"), sem("x2_kept_done")
        fq_sum_done, gate_sum_done, x1_used = sem("fq_sum_done"), sem("gate_sum_done"), sem("x1_used")

        lin_ready, sc_ready, pt_ready = ([sem(f"{n}_ready{i}") for i in range(2)] for n in ("lin", "sc", "pt"))

        lin_read = {"xT": (x_t_done, 1), "cT": (c_t_done, 1), "xk": (xk_done, 1), "xv": (xv_done, 1),
                    "y": (x_used, 1), "x1T": (x1_t_done, 1), "xq": (xq_done, 1), "x2T": (x2_t_done, 1),
                    "fq": (fq_sum_done, 1), "fk": (fk_low_done, 1), "fv": (fv_done, 1), "cross_values": (x1_used, 1), "hT": (h_t_done, 1), "fqT": (fq_low_done, 1),
                    "gate": (gate_sum_done, 1), "ffn": (ffn_read, 1)}
        for t in range(T):
            lin_read |= {("qk", t, j): (halves_done, t * 2 * CHUNKS + j + 1) for j in range(2 * CHUNKS)}
            lin_read |= {("v", t, j): (v1_done, t * CHUNKS + j + 1) for j in range(CHUNKS)}
        lin_read |= {("pair", p): (pair_done, p + 1) for p in range(PAIRS)}

        rot_flat, v_flat = (tile[:, :, :].rearrange("p t n -> p (t n)") for tile in (qk_rot, v1))
        pieces = [(rot_flat[:, 0:3 * E1], 0, 0, 3 * E1), (rot_flat[:, 3 * E1:4 * E1], 1, 0, E1),
                  (v_flat[:, 0:2 * E1], 1, E1, 2 * E1)]
        n_later = 0
        with nc.Block() as block:
            @block.sync
            def _(sp):
                nonlocal n_later
                for staged, k, at, n in pieces:
                    sp.dma_start(staged, w_qkv[k * P:(k + 1) * P, at:at + n]).then_inc(w_qkv_loaded, 16)
                sp.dma_start(x_in[:, :, :], x[0].rearrange("(t p) c -> p t c", p=P)).then_inc(x_loaded, 16)
                for dst, src in ((ident[:, :], identity), (rope_s[:, :, :, :, :], rope), (mask_s[:, :], mask)):
                    sp.dma_start(dst, src).then_inc(tables_loaded, 16)
                loads = [(temp_s[:, :], temperature.partition_broadcast(P)),
                         (wout_s[:, :, :], w_out.rearrange("(k p) n -> p k n", p=P)),
                         (gate_ws[:, :, :], gate_w.rearrange("(k p) n -> p k n", p=P))]
                for tile, w in zip(square.values(), (xwq, xwk, xwv, fwq, fwk, fwv, fwp)):
                    loads.append((tile[:, :, :], w.rearrange("(k p) n -> p k n", p=P)))
                for tile, v in zip(row.values(), (xbv, fbq, fbv, fbp, query_embedding)):
                    loads.append((tile[:, :], v.partition_broadcast(P)))
                loads.append((gate_bs[:, :], gate_b.partition_broadcast(P)))
                for tile, v in zip(column.values(), (xbq, xbk, fbk)):
                    loads.append((tile[:, :], v))
                for dst, src in loads:
                    sp.dma_start(dst, src).then_inc(w_loaded, 16)
                n_later = len(loads)
                sp.sem_inc(out_stored, 16)
                sp.dma_start(x_again[:, :, :], x[0].rearrange("(t p) c -> p t c", p=P)).then_inc(x_again_loaded, 16)
                sp.dma_start(c_in[:, :, :], ctx_in[0].rearrange("(t p) c -> p t c", p=P)).then_inc(c_loaded, 16)

            @block.scalar
            def _(act):
                act.wait_ge(w_qkv_loaded, 16 * len(pieces))
                for staged, k, at, n in pieces:
                    nc.scalar.activation(wqkv_high[:, k, at:at + n], staged, ACT.Copy).then_inc(setup_high, 1)

            @block.vector
            def _(dve):
                nc.vector.memset(v_parts[:, :, :, VW - 1:VW], 1.0)
                nc.vector.memset(power[:, :], -0.5)
                for i, (staged, k, at, n) in enumerate(pieces):
                    dve.wait_ge(setup_high, i + 1)
                    nc.vector.tensor_tensor(wqkv_low[:, k, at:at + n], staged, wqkv_high[:, k, at:at + n].bitcast(F32),
                                            ALU.subtract)
                dve.wait_ge(tables_loaded, 16 * 3)
                nc.vector.tensor_copy(ident16[:, :], ident[:, :])
        nc.all_engine_barrier()

        def turn(b, first, middle, attend, last):
            script, heads = turn_script(first, middle, attend, last)
            index = {head: n for n, head in enumerate(heads)}
            lin = Ring(lin_banks, lin_ready, [LIN_STEPS.get(s, s) for s in script if LIN_STEPS.get(s, s) in lin_read], lin_read)
            sc = Ring(sc_banks, sc_ready, heads, {h: (max_done if h[0] == "self" else exp_done, n + 1)
                                                  for n, h in enumerate(heads)})
            normalised = [h for h in heads if h[0] != "moh"]
            norm_index = {head: n for n, head in enumerate(normalised)}

            def transposed_out(head):
                return (p_parts_t_done, head[1] + 1) if head[0] == "moh" else (probs_t_done, norm_index[head] + 1)

            counted = [h for h in heads if h[0] != "cross"]
            value_index = {head: n for n, head in enumerate(counted)}

            def values_done(head):
                return lin.is_ready("cross_values") if head[0] == "cross" else (head_done, value_index[head] + 1)

            pt = Ring(pt_banks, pt_ready, heads, {h: transposed_out(h) for h in heads})

            def by_head(tile):
                return tile[:, :, :].rearrange("p t (h d) -> p t h d", d=D3)

            def v_part(i):
                return v_parts[:, :, :, i * D3:(i + 1) * D3]

            with nc.Block() as block:
                @block.sync
                def _(sp):
                    def load_next_context():
                        sp.wait_ge(c_t_done, 1)
                        sp.dma_start(c_in[:, :, :], ctx_in[b].rearrange("(t p) c -> p t c", p=P)).then_inc(c_loaded, 16)

                    def load_again():
                        sp.wait_ge(x_used, 1)
                        sp.dma_start(x_again[:, :, :], x[b].rearrange("(t p) c -> p t c", p=P)).then_inc(x_again_loaded, 16)

                    def load_next_rows():
                        sp.wait_ge(x_t_done, 1)
                        sp.dma_start(x_in[:, :, :], x[b + 1].rearrange("(t p) c -> p t c", p=P)).then_inc(x_loaded, 16)

                    def stack_parts(g, dst, parts, high_done, low_done, done):
                        if g == 0:
                            sp.wait_ge(high_done, 1)
                            sp.wait_ge(low_done, 1)
                        if attend:
                            sp.wait_ge(*sc.is_ready(("moh", KC * g + KC - 1)))
                        slot = head_slot(KC * g)
                        for i, part in enumerate(parts):
                            at = head_rows(KC * g).start + i * D3
                            sp.dma_start(dst[at:at + D3, slot:slot + KC, :].bitcast(F32),
                                         part[g * D3:(g + 1) * D3, :, :].bitcast(F32)).then_inc(done, 16)

                    for step in script:
                        if step == "cT" and first:
                            load_next_context()
                        elif step == "xT" and not (isinstance(b, int) and b == B - 1):
                            load_next_rows()
                        elif step == "z1" and first:
                            load_again()
                        elif step == "norm3":
                            sp.wait_ge(layer_done[2], 1)
                            sp.dma_start(out[b - 3].rearrange("(t p) c -> p t c", p=P), out_s[:, :, :]).then_inc(out_stored, 16)
                        elif step[0] == "stack_k":
                            stack_parts(step[1], fk_parts, (fk_high, fk_low, fk_high), fk_high_done, fk_low_done, fk_parts_done)
                        elif step[0] == "stack_q":
                            stack_parts(step[1], fq_parts, (fq_high, fq_high, fq_low), fq_high_done, fq_low_done, fq_parts_done)
                    if middle:
                        sp.wait_ge(fk_parts_done, 16 * N_STACKED)
                        sp.wait_ge(fq_parts_done, 16 * N_STACKED)

                @block.gpsimd
                def _(pool):
                    def inverse_std(n):
                        pool.wait_ge(moments_done[n], 1)
                        nc.gpsimd.tensor_scalar(var_eps[:, n, :], moments[:, n, :, 1], EPS, None, ALU.add)\
                            .then_inc(var_done[n], 1)
                        pool.wait_ge(var_done[n], 1)
                        nc.gpsimd.tensor_tensor(rstd[:, n, :], var_eps[:, n, :], power[:, 0:T], ALU.pow)\
                            .then_inc(rstd_done[n], 1)

                    for step in script:
                        if step[0] == "qk":
                            _, t, j = step
                            i = t * 2 * CHUNKS + j
                            pool.wait_ge(halves_done, i + 1)
                            tile = qk_rot[:, t, j * BANK:(j + 1) * BANK]
                            nc.gpsimd.tensor_tensor(tile, tile, rope_sin[i % 2], ALU.add).then_inc(rot_done, 1)
                        elif step[0] == "I" and step[1][0] == "moh":
                            n, h = index[step[1]], step[1][1]
                            pool.wait_ge(exp_done, n + 1)
                            if h >= HL_SLOTS:
                                pool.wait_ge(*pt.is_ready(("moh", h - HL_SLOTS)))
                            nc.gpsimd.tensor_scalar(p_high[:, h % HL_SLOTS, :], probs[:, n % P_SLOTS, :], P_SCALE, 1.0,
                                                    ALU.mult, ALU.mult).then_inc(p_high_done, 1)
                        elif step[0] == "I":
                            head = step[1]
                            n = index[head]
                            pool.wait_ge(inv_done, norm_index[head] + 1)
                            for t, (lo, hi) in enumerate([(0, P), (P, 3 * P)] if head[0] == "self" else [(0, N), (N, 2 * N)]):
                                tile = probs[:, n % P_SLOTS, lo:hi]
                                ins = nc.gpsimd.tensor_scalar(tile, tile, row_inv[:, n, t:t + 1], 1.0, ALU.mult, ALU.mult)
                            ins.then_inc(norm_done, 1)
                        elif step == "parts_of_v":
                            pool.wait_ge(v_high_done, 1)
                            nc.gpsimd.tensor_tensor(by_head(fv_rest), by_head(fv), v_part(0), ALU.subtract)\
                                .then_inc(v_rest_done, 1)
                            pool.wait_ge(v_rest_done, 1)
                            pool.wait_ge(v_mid_done, 1)
                            nc.gpsimd.tensor_tensor(v_part(2), by_head(fv_rest), v_part(1), ALU.subtract)\
                                .then_inc(v_parts_done, 1)
                        elif step in ("z1", "z2", "z3"):
                            inverse_std(int(step[1]) - 1)
                        elif step[0] == "power":
                            pool.wait_ge(ss_done, 1)
                            some = slice(step[1] * POW_COLUMNS, (step[1] + 1) * POW_COLUMNS)
                            nc.gpsimd.tensor_tensor(q_inv[:, some], q_ss[:, some], power[:, some], ALU.pow)\
                                .then_inc(q_inv_done, 1)

                @block.tensor
                def _(pe):
                    def transposed(item, src):
                        bank = lin.take(pe, item)
                        for k in range(KC):
                            for t in range(T):
                                ins = nc.tensor.transpose(bank[:, k * N + t * P:k * N + (t + 1) * P],
                                                          src[:, t, k * P:(k + 1) * P], ident[:, :])
                        ins.then_inc(lin.filled(item), 1)

                    def by_row(item, src_t, w, width):
                        bank = lin.take(pe, item)
                        for t in range(T):
                            for k in range(KC):
                                ins = nc.tensor.matmul(bank[:, t * C:t * C + width], src_t[:, k, t * P:(t + 1) * P],
                                                       w[:, k, 0:width], start=(k == 0), stop=(k == KC - 1))
                        ins.then_inc(lin.filled(item), 1)

                    def by_column(item, src_t, w):
                        bank = lin.take(pe, item)
                        for a in range(KC):
                            for k in range(KC):
                                ins = nc.tensor.matmul(bank[:, a * N:(a + 1) * N], w[:, k, a * P:(a + 1) * P],
                                                       src_t[:, k, :], start=(k == 0), stop=(k == KC - 1))
                        ins.then_inc(lin.filled(item), 1)

                    def head_scores(head):
                        kind, h = head
                        if kind == "self":
                            p, slot = h // 2, (h // 2) % 2
                            pe.wait_ge(pair_done, p + 1)
                            bank = sc.take(pe, head)
                            q, k = (qk_t[D1 * (h % 2):D1 * (h % 2) + D1, slot, i, :] for i in range(2))
                            nc.tensor.matmul(bank[:, 0:P], q[:, 0:P], k[:, 0:P], start=True, stop=True)
                            ins = nc.tensor.matmul(bank[:, P:3 * P], q[:, P:2 * P], k, start=True, stop=True)
                        elif kind == "cross":
                            pe.wait_ge(xk_done, 1)
                            pe.wait_ge(xq_done, 1)
                            bank = sc.take(pe, head)
                            for t in range(T):
                                for k in range(KC):
                                    ins = nc.tensor.matmul(bank[:, t * N:(t + 1) * N], xq_t[:, k, t * P:(t + 1) * P],
                                                           xk_t[:, k, :], start=(k == 0), stop=(k == KC - 1))
                        else:
                            bank = sc.take(pe, head)
                            for t in range(T):
                                ins = nc.tensor.matmul(bank[:, t * N:(t + 1) * N],
                                                       fq_parts[head_rows(h), head_slot(h), t * P:(t + 1) * P],
                                                       fk_parts[head_rows(h), head_slot(h), :], start=True, stop=True)
                        ins.then_inc(sc.filled(head), 1)

                    def parts_transposed(head):
                        h = head[1]
                        pe.wait_ge(p_high_done, h + 1)
                        pe.wait_ge(p_low_done, h + 1)
                        bank = pt.take(pe, head)[:, :].bitcast(F16)
                        for i, part in enumerate((p_high, p_low)):
                            for k in range(T):
                                for t in range(T):
                                    dst = (i * T + k) * N + t * P
                                    ins = nc.tensor.transpose(bank[:, dst:dst + P],
                                                              part[:, h % HL_SLOTS, t * N + k * P:t * N + (k + 1) * P],
                                                              ident16[:, :])
                        ins.then_inc(pt.filled(head), 1)

                    def head_transposed(head):
                        if head[0] == "moh":
                            return parts_transposed(head)
                        n = index[head]
                        tile = probs[:, n % P_SLOTS, :]
                        pe.wait_ge(norm_done, norm_index[head] + 1)
                        bank = pt.take(pe, head)
                        if head[0] == "self":
                            blocks = [(0, 0), (P, P), (2 * P, 2 * P)]
                        else:
                            blocks = [(k * N + t * P, t * N + k * P) for k in range(T) for t in range(T)]
                        for dst, src in blocks:
                            ins = nc.tensor.transpose(bank[:, dst:dst + P], tile[:, src:src + P], ident[:, :])
                        ins.then_inc(pt.filled(head), 1)

                    def head_values(head):
                        kind, h = head
                        n = index[head]
                        tile = probs_t[:, n % PT_SLOTS, :]
                        pe.wait_ge(*transposed_out(head))
                        if kind == "self":
                            if h == 0:
                                pe.wait_ge(v1_done, T * CHUNKS)
                            elif h % 2 == 0:
                                pe.wait_ge(o_t_done, h // 2)
                            rows = pv_self[D1 * (h % 2):D1 * (h % 2) + D1, :]
                            nc.tensor.matmul(rows[:, 0:N], v1[:, 0, h * D1:(h + 1) * D1], tile[:, 0:N],
                                             start=True, stop=False)
                            ins = nc.tensor.matmul(rows[:, P:N], v1[:, 1, h * D1:(h + 1) * D1], tile[:, N:N + P],
                                                   start=False, stop=True)
                        elif kind == "cross":
                            pe.wait_ge(xv_done, 1)
                            bank = lin.take(pe, "cross_values")
                            for t in range(T):
                                for k in range(T):
                                    ins = nc.tensor.matmul(bank[:, t * C:(t + 1) * C],
                                                           tile[:, k * N + t * P:k * N + (t + 1) * P], xv[:, k, :],
                                                           start=(k == 0), stop=(k == T - 1))
                        else:
                            if h == 0:
                                pe.wait_ge(v_parts_done, 1)
                            elif h % GH == 0:
                                pe.wait_ge(h_read, h // GH)
                            parts_t = tile.bitcast(F16)
                            for t in range(T):
                                at = (t * GH + group_column(h)) * VW
                                for j in range(2 * T):
                                    block_at = j * N + t * P
                                    ins = nc.tensor.matmul(pv_other[:, at:at + VW],
                                                           parts_t[:, block_at:block_at + P],
                                                           v_parts[:, j % T, head_of(h), :], start=(j == 0), stop=(j == 2 * T - 1))
                        ins.then_inc(lin.filled("cross_values") if kind == "cross" else head_done, 1)

                    for step in script:
                        if step == "xT":
                            pe.wait_ge(x_loaded, (b + 1) * 16)
                            transposed("xT", x_in)
                        elif step == "hT":
                            transposed("hT", h_rows)
                        elif step == "gate":
                            pe.wait_ge(h_t_done, 1)
                            by_row("gate", h_t, gate_ws, NG)
                        elif step == "ffn":
                            by_row("ffn", h_t, square["fwp"], C)
                        elif step == "x1T":
                            pe.wait_ge(layer_done[0], 1)
                            transposed("x1T", x1)
                        elif step == "cT":
                            pe.wait_ge(c_loaded, b * 16)
                            transposed("cT", c_in)
                        elif step[0] in ("qk", "v"):
                            kind, t, j = step
                            base = j * BANK + (2 * E1 if kind == "v" else 0)
                            pe.wait_ge(x_t_done, 1)
                            bank = lin.take(pe, step)
                            for i, (mine, w) in enumerate(SPLIT_PRODUCTS):
                                for k in range(KC):
                                    ins = nc.tensor.matmul(bank[:, :], (x_t_high, x_t_low)[mine][:, k, t * P:(t + 1) * P],
                                                           (wqkv_high, wqkv_low)[w][:, k, base:base + BANK],
                                                           start=(i == 0 and k == 0), stop=(i == 2 and k == KC - 1))
                            ins.then_inc(lin.filled(step), 1)
                        elif step == "xk":
                            pe.wait_ge(c_t_done, 1)
                            by_column("xk", c_t, square["xwk"])
                        elif step == "xv":
                            by_row("xv", c_t, square["xwv"], C)
                        elif step == "xq":
                            pe.wait_ge(x1_t_done, 1)
                            by_column("xq", x1_t, square["xwq"])
                        elif step == "x2T":
                            pe.wait_ge(layer_done[1], 1)
                            transposed("x2T", x2)
                        elif step == "fq":
                            pe.wait_ge(x2_t_done, 1)
                            by_row("fq", x2_t, square["fwq"], C)
                        elif step == "fk":
                            by_column("fk", x2_t, square["fwk"])
                        elif step == "fv":
                            by_row("fv", x2_t, square["fwv"], C)
                        elif step == "fqT":
                            pe.wait_ge(fq_done, 1)
                            transposed("fqT", fq)
                        elif step[0] == "pair":
                            p = step[1]
                            pe.wait_ge(rot_done, 2 * CHUNKS + CHUNKS + p // 4 + 1)
                            bank = lin.take(pe, step)
                            for i in range(2):
                                for t in range(T):
                                    ins = nc.tensor.transpose(bank[:, i * N + t * P:i * N + (t + 1) * P],
                                                              qk_rot[:, t, i * E1 + p * P:i * E1 + (p + 1) * P], ident[:, :])
                            ins.then_inc(lin.filled(step), 1)
                        elif step in ("y", "y_rest"):
                            t = 0 if step == "y" else 1
                            bank = lin.take(pe, "y") if t == 0 else lin.bank("y")
                            for p in range(PAIRS):
                                ins = nc.tensor.matmul(bank[:, t * C:(t + 1) * C], o_t[:, p, t * P:(t + 1) * P],
                                                       wout_s[:, p, :], start=(p == 0), stop=(p == PAIRS - 1))
                            if t == 1:
                                ins.then_inc(lin.filled("y"), 1)
                        elif step[0] == "S":
                            head_scores(step[1])
                        elif step[0] == "T":
                            head_transposed(step[1])
                        elif step[0] == "V":
                            head_values(step[1])

                @block.scalar
                def _(act):
                    def copy(dst, item, done):
                        act.wait_ge(*lin.is_ready(item))
                        nc.scalar.activation(dst, lin.bank(item)[:, :], ACT.Copy).then_inc(done, 1)

                    def two(tile):
                        return tile[:, :, :].rearrange("p a n -> p (a n)")

                    def biased(dst, item, bias, done):
                        act.wait_ge(*lin.is_ready(item))
                        for a in range(KC):
                            ins = nc.scalar.activation(dst[:, a, :], lin.bank(item)[:, a * N:(a + 1) * N],
                                                       ACT.Identity, bias=bias[:, a:a + 1])
                        ins.then_inc(done, 1)

                    def pair(p):
                        item, slot = ("pair", p), p % 2
                        act.wait_ge(*lin.is_ready(item))
                        if p >= 2:
                            for h in (2 * (p - 2), 2 * (p - 2) + 1):
                                act.wait_ge(*sc.is_ready(("self", h)))
                        nc.scalar.activation(qk_t[:, slot, :, :].rearrange("p i n -> p (i n)"), lin.bank(item)[:, :],
                                             ACT.Copy).then_inc(pair_done, 1)

                    def head_exp(head):
                        n = index[head]
                        act.wait_ge(max_done, n + 1)
                        if n >= P_SLOTS:
                            before = heads[n - P_SLOTS]
                            if before[0] == "moh":
                                act.wait_ge(p_low_done, before[1] + 1)
                            else:
                                act.wait_ge(*pt.is_ready(before))
                        if head[0] == "self":
                            parts = [(scores[:, n % S_SLOTS, lo:hi], lo, hi) for lo, hi in ((0, P), (P, 3 * P))]
                            sign = -1.0
                        else:
                            parts = [(sc.bank(head)[:, t * N:(t + 1) * N], t * N, (t + 1) * N) for t in range(T)]
                            sign = 1.0
                        for t, (src, lo, hi) in enumerate(parts):
                            tile, shift = probs[:, n % P_SLOTS, lo:hi], neg_max[:, n, t:t + 1]
                            if head[0] == "moh":
                                ins = nc.scalar.activation(tile, src, ACT.Exp, bias=shift, scale=sign)
                            else:
                                ins = nc.scalar.activation(tile, src, ACT.Exp, bias=shift, scale=sign,
                                                           accum_out=row_sum[:, n, t:t + 1])
                        ins.then_inc(exp_done, 1)

                    for step in script:
                        if step == "keep":
                            if last:
                                act.wait_ge(ffn_read, 1)
                            nc.scalar.activation(x2_kept[:, :, :], x2, ACT.Copy).then_inc(x2_kept_done, 1)
                        elif step == "xT":
                            copy(two(x_t_high), "xT", x_high_done)
                        elif step == "cT":
                            copy(two(c_t), "cT", c_t_done)
                        elif step == "hT":
                            copy(two(h_t), "hT", h_t_done)
                        elif step == "x1T":
                            copy(two(x1_t), "x1T", x1_t_done)
                        elif step == "x2T":
                            copy(two(x2_t), "x2T", x2_t_done)
                        elif step == "fqT":
                            copy(two(fq_high), "fqT", fq_high_done)
                        elif step[0] == "v":
                            _, t, j = step
                            copy(v1[:, t, j * BANK:(j + 1) * BANK], step, v1_done)
                        elif step == "xk":
                            biased(xk_t, "xk", column["xbk"], xk_done)
                        elif step == "fk":
                            biased(fk_high, "fk", column["fbk"], fk_high_done)
                        elif step[0] == "pair_out":
                            pair(step[1])
                        elif step == "parts_of_v":
                            nc.scalar.activation(v_part(0), by_head(fv), ACT.Copy).then_inc(v_high_done, 1)
                            act.wait_ge(v_rest_done, 1)
                            nc.scalar.activation(v_part(1), by_head(fv_rest), ACT.Copy).then_inc(v_mid_done, 1)
                        elif step[0] == "S":
                            head_exp(step[1])
                        elif step[0] == "E" and step[1][0] == "moh":
                            n = index[step[1]]
                            act.wait_ge(*pt.is_ready(step[1]))
                            if n >= PT_SLOTS:
                                act.wait_ge(*values_done(heads[n - PT_SLOTS]))
                            nc.scalar.activation(probs_t[:, n % PT_SLOTS, :].bitcast(F16), pt.bank(step[1])[:, :].bitcast(F16),
                                                 ACT.Copy).then_inc(p_parts_t_done, 1)
                        elif step == "logits":
                            act.wait_ge(logits_done, 1)
                            nc.scalar.activation(gates[:, 2, :, :], gates[:, 1, :, :], ACT.Exp).then_inc(gate_exp_done, 1)
                        elif step[0] == "O":
                            kind, h = step[1]
                            if kind == "self" and h % 2 == 1:
                                act.wait_ge(*values_done(step[1]))
                                nc.scalar.activation(o_t[:, h // 2, :], pv_self[:, 0:N], ACT.Copy).then_inc(o_t_done, 1)

                @block.vector
                def _(dve):
                    count = [0]

                    def mark(ins):
                        count[0] += 1
                        return ins.then_inc(dve_step, 1)

                    def settled():
                        dve.wait_ge(dve_step, count[0])

                    def both(bank):
                        return bank[:, :].rearrange("p (t c) -> p t c", t=T)

                    def rows_of(r):
                        return r[:, :].rearrange("p (o c) -> p o c", o=1).to_broadcast([P, T, C])

                    def rotate(step):
                        _, t, j = step
                        i = t * 2 * CHUNKS + j
                        dve.wait_ge(*lin.is_ready(step))
                        if i >= 2:
                            dve.wait_ge(rot_done, i - 1)
                        bank = lin.bank(step)[:, :].rearrange("p (h s d) -> p h s d", s=2, d=D1 // 2)
                        shape = [P, BANK // D1, 2, D1 // 2]
                        cos, sin = (rope_s[:, t, j // CHUNKS, f, :].rearrange("p (o s d) -> p o s d", o=1, s=2).to_broadcast(shape)
                                    for f in range(2))
                        dst = [r.rearrange("p (h s d) -> p h s d", s=2, d=D1 // 2)
                               for r in (qk_rot[:, t, j * BANK:(j + 1) * BANK], rope_sin[i % 2])]
                        nc.vector.tensor_tensor(dst[0], bank, cos, ALU.mult)
                        nc.vector.tensor_tensor(dst[1], bank[:, :, ::-1, :], sin, ALU.mult).then_inc(halves_done, 1)

                    def head_max(head):
                        n = index[head]
                        dve.wait_ge(*sc.is_ready(head))
                        bank = sc.bank(head)
                        if head[0] == "self":
                            if n >= S_SLOTS:
                                dve.wait_ge(exp_done, n - S_SLOTS + 1)
                            for t, (lo, hi) in enumerate(((0, P), (P, 3 * P))):
                                ins = nc.vector.tensor_tensor_reduce(
                                    out=scores[:, n % S_SLOTS, lo:hi], in0=bank[:, lo:hi], in1=mask_s[:, lo:hi],
                                    scale=-1.0, scalar=3.4e38, op0=ALU.add, op1=ALU.min,
                                    accum_out=neg_max[:, n, t:t + 1])
                            ins.then_inc(max_done, 1)
                        else:
                            nc.vector.tensor_reduce(neg_max[:, n, :], bank[:, :].rearrange("p (t n) -> p t n", t=T),
                                                    AX.X, ALU.max, negate=True).then_inc(max_done, 1)

                    def head_evacuate(head):
                        n = index[head]
                        width = 3 * P if head[0] == "self" else 2 * N
                        dve.wait_ge(*pt.is_ready(head))
                        if n >= PT_SLOTS:
                            dve.wait_ge(*values_done(heads[n - PT_SLOTS]))
                        nc.vector.tensor_copy(probs_t[:, n % PT_SLOTS, 0:width], pt.bank(head)[:, 0:width])\
                            .then_inc(probs_t_done, 1)

                    def moments_of(n):
                        for t in range(T):
                            mark(nc.vector.bn_stats(stats[:, n, t, :], z[:, n, t, :]))
                        settled()
                        for t in range(T):
                            ins = nc.vector.bn_aggr(moments[:, n, t, :], stats[:, n, t, :])
                        ins.then_inc(moments_done[n], 1)

                    def normed(n, dst):
                        dve.wait_ge(moments_done[n], 1)
                        dve.wait_ge(rstd_done[n], 1)
                        for t in range(T):
                            ins = nc.vector.tensor_scalar(dst[:, t, :], z[:, n, t, :], moments[:, n, t, 0:1],
                                                          rstd[:, n, t:t + 1], ALU.subtract, ALU.mult)
                        ins.then_inc(layer_done[n], 1)

                    heads_of = "p t (h d) -> p t h d"
                    per_head = [P, T, H3, D3]

                    def squares():
                        dve.wait_ge(fq_sum_done, 1)
                        if attend:
                            dve.wait_ge(v_parts_done, 1)
                        mark(nc.vector.tensor_tensor(fv[:, :, :], fq[:, :, :], fq[:, :, :], ALU.mult))
                        settled()
                        nc.vector.tensor_reduce(q_ss[:, :], fv[:, :, :].rearrange("p t (h d) -> p (t h) d", d=D3),
                                                AX.X, ALU.add).then_inc(ss_done, 1)

                    def scaled_queries():
                        dve.wait_ge(q_inv_done, POW_STEPS)
                        inv = q_inv[:, :].rearrange("p (t h o) -> p t h o", t=T, o=1).to_broadcast(per_head)
                        mark(nc.vector.tensor_tensor(fq[:, :, :].rearrange(heads_of, h=H3),
                                                     fq[:, :, :].rearrange(heads_of, h=H3), inv, ALU.mult))
                        settled()
                        mark(nc.vector.tensor_tensor(fq[:, :, :], fq[:, :, :], rows_of(row["qe"]), ALU.add))
                        settled()
                        scale = head_scale[:, :].rearrange("p (u h o) -> p u h o", u=1, o=1).to_broadcast(per_head)
                        nc.vector.tensor_tensor(fq[:, :, :].rearrange(heads_of, h=H3),
                                                fq[:, :, :].rearrange(heads_of, h=H3), scale, ALU.mult).then_inc(fq_done, 1)

                    def group_outputs(h):
                        dve.wait_ge(*values_done(("moh", h)))
                        if h >= GH:
                            dve.wait_ge(h_rows_done, h // GH)
                        bank = pv_other[:, 0:T * GH * VW].rearrange("p (g c) -> p g c", c=VW)
                        mark(nc.vector.tensor_reduce(h_sum[:, :, :], bank[:, :, 0:PARTS * D3].rearrange(
                            "p g (c d) -> p g d c", d=D3), AX.X, ALU.add))
                        nc.vector.reciprocal(h_inv[:, :], bank[:, :, VW - 1]).then_inc(h_read, 1)
                        settled()
                        dve.wait_ge(h_read, h // GH + 1)
                        near = GH // KC
                        first = h // GH * near * D3
                        nc.vector.tensor_tensor(
                            h_rows[:, :, :].rearrange("p t (k c) -> p (t k) c", k=KC)[:, :, first:first + near * D3]
                            .rearrange("p a (h d) -> p a h d", d=D3),
                            h_sum[:, :, :].rearrange("p (a h) d -> p a h d", h=near),
                            h_inv[:, :].rearrange("p (a h o) -> p a h o", h=near, o=1).to_broadcast([P, T * KC, near, D3]),
                            ALU.mult).then_inc(h_rows_done, 1)

                    routed, shared = slice(0, NR), slice(NR, NG)

                    def small(i):
                        return gsmall[:, i, :]

                    def wide(i, n):
                        return gsmall[:, i, :].rearrange("p (t o) -> p t o", o=1).to_broadcast([P, T, n])

                    def gate_logits():
                        dve.wait_ge(*lin.is_ready("gate"))
                        nc.vector.tensor_tensor(gates[:, 0, :, :], both(lin.bank("gate"))[:, :, 0:NG],
                                                gate_bs[:, :].rearrange("p (o c) -> p o c", o=1).to_broadcast([P, T, NG]),
                                                ALU.add).then_inc(gate_sum_done, 1)
                        dve.wait_ge(gate_sum_done, 1)
                        mark(nc.vector.tensor_reduce(small(0), gates[:, 0, :, routed], AX.X, ALU.max))
                        mark(nc.vector.tensor_reduce(small(1), gates[:, 0, :, shared], AX.X, ALU.max))
                        settled()
                        nc.vector.tensor_tensor(gates[:, 1, :, routed], gates[:, 0, :, routed], wide(0, NR), ALU.subtract)
                        nc.vector.tensor_tensor(gates[:, 1, :, shared], gates[:, 0, :, shared], wide(1, NS), ALU.subtract)\
                            .then_inc(logits_done, 1)

                    def gate_factor():
                        dve.wait_ge(gate_exp_done, 1)
                        mark(nc.vector.tensor_reduce(small(2), gates[:, 2, :, routed], AX.X, ALU.add))
                        mark(nc.vector.tensor_reduce(small(3), gates[:, 2, :, shared], AX.X, ALU.add))
                        settled()
                        mark(nc.vector.reciprocal(gsmall[:, 4:6, :], gsmall[:, 2:4, :]))
                        settled()
                        mark(nc.vector.tensor_tensor(gates[:, 3, :, routed], gates[:, 2, :, routed], wide(4, NR), ALU.mult))
                        mark(nc.vector.tensor_tensor(gates[:, 3, :, shared], gates[:, 2, :, shared], wide(5, NS), ALU.mult))
                        settled()
                        for t in range(T):
                            mark(nc.vector.max(top8[:, t, :], gates[:, 3, t, routed]))
                        mark(nc.vector.tensor_reduce(small(6), gates[:, 3, :, shared], AX.X, ALU.add))
                        settled()
                        mark(nc.vector.tensor_reduce(small(7), top8[:, :, 0:TOPK], AX.X, ALU.add))
                        mark(nc.vector.tensor_tensor(small(8), gates[:, 3, :, NR], small(6), ALU.mult))
                        settled()
                        mark(nc.vector.scalar_tensor_tensor(small(9), small(7), float(TOPK), gates[:, 3, :, NR + 1],
                                                            ALU.mult, ALU.mult))
                        settled()
                        mark(nc.vector.tensor_tensor(small(10), small(8), small(9), ALU.add))
                        settled()
                        mark(nc.vector.tensor_scalar(small(11), small(10), 2.0, None, ALU.mult))

                    def scaled_projection():
                        settled()
                        dve.wait_ge(*lin.is_ready("ffn"))
                        dve.wait_ge(out_stored, (b - 2) * 16)
                        for t in range(T):
                            ins = nc.vector.scalar_tensor_tensor(z[:, 2, t, :], lin.bank("ffn")[:, t * C:(t + 1) * C],
                                                                 gsmall[:, 11, t:t + 1], x2_kept[:, t, :], ALU.mult, ALU.add)
                        ins.then_inc(ffn_read, 1)

                    def low_part(low, item, high, high_done, done):
                        dve.wait_ge(*lin.is_ready(item))
                        dve.wait_ge(high_done, 1)
                        nc.vector.tensor_tensor(low[:, :, :], both(lin.bank(item)), high[:, :, :].bitcast(F32),
                                                ALU.subtract).then_inc(done, 1)

                    for step in script:
                        if step == "xT":
                            low_part(x_t_low, "xT", x_t_high, x_high_done, x_t_done)
                        elif step[0] == "qk":
                            rotate(step)
                        elif step == "xv":
                            dve.wait_ge(*lin.is_ready("xv"))
                            nc.vector.tensor_tensor(xv[:, :, :], both(lin.bank("xv")), rows_of(row["xbv"]), ALU.add)\
                                .then_inc(xv_done, 1)
                        elif step == "xq":
                            dve.wait_ge(*lin.is_ready("xq"))
                            for a in range(KC):
                                ins = nc.vector.tensor_scalar(xq_t[:, a, :], lin.bank("xq")[:, a * N:(a + 1) * N],
                                                              column["xbq"][:, a:a + 1], float(C) ** -0.5, ALU.add, ALU.mult)
                            ins.then_inc(xq_done, 1)
                        elif step == "logits":
                            gate_logits()
                        elif step == "factor":
                            gate_factor()
                        elif step == "sum3":
                            scaled_projection()
                        elif step == "z1":
                            dve.wait_ge(*lin.is_ready("y"))
                            dve.wait_ge(x_again_loaded, b * 16)
                            nc.vector.tensor_tensor(z[:, 0, :, :], both(lin.bank("y")), x_again[:, :, :], ALU.add)\
                                .then_inc(x_used, 1)
                            dve.wait_ge(x_used, 1)
                            moments_of(0)
                        elif step == "z2":
                            dve.wait_ge(*lin.is_ready("cross_values"))
                            if attend:
                                dve.wait_ge(x2_kept_done, 1)
                            nc.vector.tensor_tensor(z[:, 1, :, :], both(lin.bank("cross_values")), x1, ALU.add).then_inc(x1_used, 1)
                            dve.wait_ge(x1_used, 1)
                            moments_of(1)
                        elif step == "z3":
                            dve.wait_ge(ffn_read, 1)
                            mark(nc.vector.tensor_tensor(z[:, 2, :, :], z[:, 2, :, :], rows_of(row["fbp"]), ALU.add))
                            settled()
                            moments_of(2)
                        elif step == "norm1":
                            normed(0, x1)
                        elif step == "norm2":
                            normed(1, x2)
                        elif step == "norm3":
                            normed(2, out_s)
                        elif step == "fq":
                            dve.wait_ge(*lin.is_ready("fq"))
                            nc.vector.tensor_tensor(fq[:, :, :], both(lin.bank("fq")), rows_of(row["fbq"]), ALU.add)\
                                .then_inc(fq_sum_done, 1)
                        elif step == "fk":
                            dve.wait_ge(*lin.is_ready("fk"))
                            dve.wait_ge(fk_high_done, 1)
                            for a in range(KC):
                                ins = nc.vector.scalar_tensor_tensor(
                                    fk_low[:, a, :], lin.bank("fk")[:, a * N:(a + 1) * N], column["fbk"][:, a:a + 1],
                                    fk_high[:, a, :].bitcast(F32), ALU.add, ALU.subtract)
                            ins.then_inc(fk_low_done, 1)
                        elif step == "fqT":
                            low_part(fq_low, "fqT", fq_high, fq_high_done, fq_low_done)
                        elif step == "fv":
                            dve.wait_ge(*lin.is_ready("fv"))
                            dve.wait_ge(ss_done, 1)
                            nc.vector.tensor_tensor(fv[:, :, :], both(lin.bank("fv")), rows_of(row["fbv"]), ALU.add)\
                                .then_inc(fv_done, 1)
                        elif step == "fq_squares":
                            squares()
                        elif step == "fq_scaled":
                            scaled_queries()
                        elif step[0] == "S":
                            head_max(step[1])
                        elif step[0] == "L" and step[1][0] == "moh":
                            n, h = index[step[1]], step[1][1]
                            dve.wait_ge(p_high_done, h + 1)
                            if h >= HL_SLOTS:
                                dve.wait_ge(*pt.is_ready(("moh", h - HL_SLOTS)))
                            nc.vector.scalar_tensor_tensor(p_low[:, h % HL_SLOTS, :], probs[:, n % P_SLOTS, :], P_SCALE,
                                                           p_high[:, h % HL_SLOTS, :], ALU.mult, ALU.subtract)\
                                .then_inc(p_low_done, 1)
                        elif step[0] == "G":
                            if step[1][0] == "moh" and step[1][1] % GH == GH - 1:
                                group_outputs(step[1][1])
                        elif step[0] == "I" and step[1][0] != "moh":
                            n = index[step[1]]
                            dve.wait_ge(exp_done, n + 1)
                            nc.vector.reciprocal(row_inv[:, n, :], row_sum[:, n, :]).then_inc(inv_done, 1)
                        elif step[0] == "E" and step[1][0] != "moh":
                            head_evacuate(step[1])

            nc.all_engine_barrier(sems_to_clear=range(dve_step.num, pt_ready[-1].num + 1))

        turn(0, True, False, False, False)

        with nc.Block() as block:
            @block.vector
            def _(dve):
                count = [0]

                def step(ins):
                    count[0] += 1
                    ins.then_inc(setup_dve, 1)
                    dve.wait_ge(setup_dve, count[0])

                u, w, ln_w, d, e, tmp = (soft[:, i, :] for i in range(6))
                dve.wait_ge(w_loaded, 16 * n_later)
                step(nc.vector.tensor_scalar(tmp, temp_s[:, :], -1.0, None, ALU.mult))
                step(nc.vector.tensor_tensor(tmp, tmp, temp_s[:, :], ALU.min))
                dve.wait_ge(setup_act, 1)
                step(nc.vector.tensor_scalar(w, u, 1.0, None, ALU.add))
                dve.wait_ge(setup_act, 2)
                step(nc.vector.tensor_scalar(d, w, 1.0, None, ALU.subtract))
                step(nc.vector.tensor_scalar(e, d, 0.0, None, ALU.is_equal))
                step(nc.vector.tensor_tensor(d, d, e, ALU.add))
                step(nc.vector.tensor_tensor(ln_w, ln_w, e, ALU.add))
                step(nc.vector.reciprocal(d, d))
                step(nc.vector.tensor_tensor(d, d, ln_w, ALU.mult))
                step(nc.vector.tensor_tensor(d, d, u, ALU.mult))
                step(nc.vector.tensor_scalar(e, temp_s[:, :], 0.0, None, ALU.max))
                step(nc.vector.tensor_tensor(d, d, e, ALU.add))
                step(nc.vector.tensor_scalar(head_scale[:, :], d, float(D3) ** -0.5, None, ALU.mult))

            @block.scalar
            def _(act):
                act.wait_ge(setup_dve, 2)
                nc.scalar.activation(soft[:, 0, :], soft[:, 5, :], ACT.Exp).then_inc(setup_act, 1)
                act.wait_ge(setup_dve, 3)
                nc.scalar.activation(soft[:, 2, :], soft[:, 1, :], ACT.Ln).then_inc(setup_act, 1)
        nc.all_engine_barrier()

        turn(1, True, True, False, False)
        turn(2, True, True, True, False)
        with nc.Fori(3, B - 1) as b:
            turn(b, True, True, True, True)
        turn(B - 1, True, True, True, True)
        turn(B, False, True, True, True)
        turn(B + 1, False, False, True, True)
        turn(B + 2, False, False, False, True)

        with nc.Block() as block:
            @block.sync
            def _(sp):
                sp.wait_ge(out_stored, 16 * (B + 1))


def kernel(**inputs):
    import numpy as np
    import concourse.bacc as bacc
    from concourse.bass_utils import run_bass_kernel_spmd

    def arr(name):
        return np.asarray(inputs[name])

    f = np.float32
    inv_freq = (f(1.0) / np.power(f(10000.0), np.arange(0, D1, 2, dtype=f) / f(D1))).astype(f)
    angle = np.arange(N, dtype=f)[:, None] * inv_freq[None, :]
    cos, sin = np.cos(angle).astype(f), np.sin(angle).astype(f)
    table = np.stack([np.concatenate([cos, cos], 1), np.concatenate([-sin, sin], 1)], 1)
    table = np.stack([table * f(D1 ** -0.5), table], 1)
    rope = np.ascontiguousarray(table.reshape(T, P, 2, 2, D1).transpose(1, 0, 2, 3, 4))
    i, j = np.arange(P)[:, None], np.arange(P)[None, :]
    causal = np.where(j <= i, f(0), f(-BIG))
    band = np.where(j >= i, f(0), f(-BIG))
    mask = np.ascontiguousarray(np.concatenate([causal, band, causal], 1).astype(f))

    def cols(a):
        return a.reshape(KC, P).T

    arrays = {
        "x": arr("x"), "ctx_in": arr("ctx_1024"), "w_qkv": arr("L0_attn_W_qkv"), "w_out": arr("L0_attn_W_out"),
        "xwq": arr("L0_xattn_Wq"), "xbq": cols(arr("L0_xattn_bq")), "xwk": arr("L0_xattn_Wk"),
        "xbk": cols(arr("L0_xattn_bk")), "xwv": arr("L0_xattn_Wv"), "xbv": arr("L0_xattn_bv"),
        "fwq": arr("L0_ffn_Wq").T, "fbq": arr("L0_ffn_bq"), "fwk": arr("L0_ffn_Wk").T, "fbk": cols(arr("L0_ffn_bk")),
        "fwv": arr("L0_ffn_Wv").T, "fbv": arr("L0_ffn_bv"), "fwp": arr("L0_ffn_Wp").T, "fbp": arr("L0_ffn_bp"),
        "gate_w": np.concatenate([arr("L0_ffn_Wr"), arr("L0_ffn_Ws")], 0).T,
        "gate_b": np.concatenate([arr("L0_ffn_br"), arr("L0_ffn_bs")], 0),
        "temperature": arr("L0_ffn_temperature").reshape(-1),
        "query_embedding": arr("L0_ffn_query_embedding").reshape(-1),
        "rope": rope, "mask": mask, "identity": np.eye(P, dtype=f),
    }
    nc = bacc.Bacc("TRN2", target_bir_lowering=False, num_devices=1)
    given, args = {}, {}
    for name, a in arrays.items():
        a = np.ascontiguousarray(a)
        given[f"in_{name}"] = a
        args[name] = nc.dram_tensor(f"in_{name}", a.shape, mybir.dt.from_np(a.dtype), kind="ExternalInput").ap()
    args["out"] = nc.dram_tensor("out_0", (B, N, C), F32, kind="ExternalOutput").ap()
    decoder_layer(nc, **args)
    r = run_bass_kernel_spmd(nc, [given], core_ids=[0])
    return r.results[0]["out_0"]
```
